# Optimizing a Trainium2 kernel written in Bass

```python
import numpy as np
import jax
import jax.numpy as jnp

def _softmax(x, axis=-1):
    return jax.nn.softmax(x, axis=axis)

def _gelu(x):
    return jax.nn.gelu(x, approximate=True)

def _silu(x):
    return jax.nn.silu(x)

def _sigmoid(x):
    return jax.nn.sigmoid(x)

def _layernorm(x, axis=-1, eps=1e-05):
    m = jnp.mean(x, axis=axis, keepdims=True)
    v = jnp.var(x, axis=axis, keepdims=True)
    return (x - m) / jnp.sqrt(v + eps)

def _scatter_add(tgt, idx, src, axis=0):
    return tgt.at[idx].add(src)

def _segment_sum(src, seg, n):
    return jax.ops.segment_sum(src, seg, n)
kernel_name = 'mk_recurrent_d1_jaxref_r8_38261d'

def setup_inputs(seed: int=0):
    np.random.seed(seed)
    _w = jnp.asarray

    def _L0_attn_setup():
        import jax, jax.numpy as jnp
        import numpy as np
        _A = np.array([[1, 1, 1, 0, 1, 1, 1, 0, 0, 0, 1, 1], [1, 1, 0, 1, 1, 1, 0, 0, 0, 1, 1, 0], [1, 0, 1, 1, 1, 0, 0, 0, 1, 1, 0, 1], [0, 1, 1, 1, 0, 0, 0, 1, 1, 0, 1, 1], [0, 0, 0, 0, 1, 1, 1, 1, 1, 1, 1, 1], [1, 1, 1, 1, 0, 0, 0, 0, 0, 0, 0, 0], [0, 0, 0, 0, 1, 1, 1, 1, 0, 0, 0, 0], [1, 1, 0, 0, 1, 1, 0, 0, 1, 1, 0, 0], [1, 0, 1, 0, 1, 0, 1, 0, 1, 0, 1, 0], [0, 1, 0, 1, 0, 1, 0, 1, 0, 1, 0, 1], [1, 0, 0, 1, 1, 0, 0, 1, 1, 0, 0, 1], [0, 1, 1, 0, 0, 1, 1, 0, 0, 1, 1, 0]], dtype=np.float32)
        _H = jnp.asarray(np.concatenate([_A.T, np.eye(12, dtype=np.float32)], axis=1))

        def _fractal_dimension(x):
            s = x.reshape(-1)
            sn = (s - s.min()) / (s.max() - s.min() + 1e-10)
            counts = []
            for sc in (2, 4, 8, 16, 32):
                blk = sn[:sc * sc]
                counts.append(jnp.maximum(jnp.sum(blk > blk.mean()).astype(jnp.float32), 1.0))
            lx = jnp.log(jnp.array([2.0, 4.0, 8.0, 16.0, 32.0], dtype=jnp.float32))
            ly = jnp.log(jnp.stack(counts))
            n = jnp.float32(5.0)
            num = n * jnp.sum(lx * ly) - jnp.sum(lx) * jnp.sum(ly)
            den = n * jnp.sum(lx * lx) - jnp.sum(lx) ** 2
            return jnp.clip(-num / den, 1.0, 2.0)

        def _wave_filter(D, d):
            k = jnp.fft.fftfreq(d).astype(jnp.float32)
            ka = jnp.abs(k) + 1e-08
            omega = 1.0 + 0.2 * D
            a = 1.0 + 0.5 * D
            b = 0.1 * D
            real = jnp.sin(omega * D + a * ka)
            phase = omega * D - ka + b * ka ** 2
            return real * jnp.exp(1j * phase)

        def _golay_correct(bits):
            syn = (bits @ _H.T > 0.5).astype(jnp.float32)
            w = syn.sum(-1)
            _, idx = jax.lax.top_k(syn, 3)
            take = (jnp.arange(3)[None, :] < jnp.minimum(w, 3.0)[:, None]).astype(jnp.float32)
            pattern = (jax.nn.one_hot(idx, 24, dtype=jnp.float32) * take[..., None]).sum(axis=1)
            do_fix = ((w > 0) & (w <= 3))[:, None]
            return jnp.where(do_fix, jnp.mod(bits + pattern, 2.0), bits)
        key = jax.random.key(seed)
        k1, k2, k3 = jax.random.split(key, 3)
        B, S, E = (8, 256, 128)
        x = jax.random.normal(k1, (B, S, E), dtype=jnp.float32)
        W_el = jax.random.normal(k2, (E, 24), dtype=jnp.float32) * 0.02
        b_el = jnp.zeros((24,), dtype=jnp.float32)
        W_le = jax.random.normal(k3, (24, E), dtype=jnp.float32) * 0.02
        b_le = jnp.zeros((E,), dtype=jnp.float32)
        return {'x': x, 'W_el': W_el, 'b_el': b_el, 'W_le': W_le, 'b_le': b_le}
    _L0_attn_in = _L0_attn_setup()

    def _L0_ffn_setup():
        import jax, jax.numpy as jnp
        import numpy as np
        H = 128
        I = 64
        E = 64
        G = 8
        TOPK_GROUP = 4
        K = 8
        I_SH = 128
        SCALE = 2.5

        def _route(x, router_w, e_bias):
            T = x.shape[0]
            scores = jax.nn.sigmoid(x.astype(jnp.float32) @ router_w.T.astype(jnp.float32))
            sfc = jax.lax.stop_gradient(scores) + e_bias[None, :]
            group_scores = jax.lax.top_k(sfc.reshape(T, G, E // G), 2)[0].sum(-1)
            _, gidx = jax.lax.top_k(group_scores, TOPK_GROUP)
            gmask = jax.nn.one_hot(gidx, G, dtype=sfc.dtype).sum(1)
            smask = jnp.repeat(gmask, E // G, axis=1)
            masked = jnp.where(smask > 0, sfc, 0.0)
            _, topk_idx = jax.lax.top_k(masked, K)
            w = jnp.take_along_axis(scores, topk_idx, axis=1)
            w = w / (w.sum(-1, keepdims=True) + 1e-20)
            return (topk_idx, w * SCALE)
        key = jax.random.key(seed)
        ks = jax.random.split(key, 9)
        s = 0.02
        return {'hidden_states': jax.random.normal(ks[0], (2, 128, H), jnp.float32), 'router_w': jax.random.normal(ks[1], (E, H), jnp.float32) * s, 'e_bias': jnp.zeros((E,), jnp.float32), 'Wg': jax.random.normal(ks[2], (E, H, I), jnp.float32) * s, 'Wu': jax.random.normal(ks[3], (E, H, I), jnp.float32) * s, 'Wd': jax.random.normal(ks[4], (E, I, H), jnp.float32) * s, 'SWg': jax.random.normal(ks[5], (H, I_SH), jnp.float32) * s, 'SWu': jax.random.normal(ks[6], (H, I_SH), jnp.float32) * s, 'SWd': jax.random.normal(ks[7], (I_SH, H), jnp.float32) * s}
    _L0_ffn_in = _L0_ffn_setup()
    _d = {'L0_attn_x': _L0_attn_in['x'], 'L0_attn_W_el': _L0_attn_in['W_el'], 'L0_attn_b_el': _L0_attn_in['b_el'], 'L0_attn_W_le': _L0_attn_in['W_le'], 'L0_attn_b_le': _L0_attn_in['b_le'], 'L0_ffn_router_w': _L0_ffn_in['router_w'], 'L0_ffn_e_bias': _L0_ffn_in['e_bias'], 'L0_ffn_Wg': _L0_ffn_in['Wg'], 'L0_ffn_Wu': _L0_ffn_in['Wu'], 'L0_ffn_Wd': _L0_ffn_in['Wd'], 'L0_ffn_SWg': _L0_ffn_in['SWg'], 'L0_ffn_SWu': _L0_ffn_in['SWu'], 'L0_ffn_SWd': _L0_ffn_in['SWd']}
    _x0 = _d['L0_attn_x']
    _d['L0_attn_x'] = jax.random.normal(jax.random.fold_in(jax.random.key(seed), 1), (16, 256, 128), dtype=_x0.dtype)
    del _x0
    return _d

def reference(L0_attn_x, L0_attn_W_el, L0_attn_b_el, L0_attn_W_le, L0_attn_b_le, L0_ffn_router_w, L0_ffn_e_bias, L0_ffn_Wg, L0_ffn_Wu, L0_ffn_Wd, L0_ffn_SWg, L0_ffn_SWu, L0_ffn_SWd):

    def _L0_attn_ref(x, W_el, b_el, W_le, b_le):
        import jax, jax.numpy as jnp
        import numpy as np
        _A = np.array([[1, 1, 1, 0, 1, 1, 1, 0, 0, 0, 1, 1], [1, 1, 0, 1, 1, 1, 0, 0, 0, 1, 1, 0], [1, 0, 1, 1, 1, 0, 0, 0, 1, 1, 0, 1], [0, 1, 1, 1, 0, 0, 0, 1, 1, 0, 1, 1], [0, 0, 0, 0, 1, 1, 1, 1, 1, 1, 1, 1], [1, 1, 1, 1, 0, 0, 0, 0, 0, 0, 0, 0], [0, 0, 0, 0, 1, 1, 1, 1, 0, 0, 0, 0], [1, 1, 0, 0, 1, 1, 0, 0, 1, 1, 0, 0], [1, 0, 1, 0, 1, 0, 1, 0, 1, 0, 1, 0], [0, 1, 0, 1, 0, 1, 0, 1, 0, 1, 0, 1], [1, 0, 0, 1, 1, 0, 0, 1, 1, 0, 0, 1], [0, 1, 1, 0, 0, 1, 1, 0, 0, 1, 1, 0]], dtype=np.float32)
        _H = jnp.asarray(np.concatenate([_A.T, np.eye(12, dtype=np.float32)], axis=1))

        def _fractal_dimension(x):
            s = x.reshape(-1)
            sn = (s - s.min()) / (s.max() - s.min() + 1e-10)
            counts = []
            for sc in (2, 4, 8, 16, 32):
                blk = sn[:sc * sc]
                counts.append(jnp.maximum(jnp.sum(blk > blk.mean()).astype(jnp.float32), 1.0))
            lx = jnp.log(jnp.array([2.0, 4.0, 8.0, 16.0, 32.0], dtype=jnp.float32))
            ly = jnp.log(jnp.stack(counts))
            n = jnp.float32(5.0)
            num = n * jnp.sum(lx * ly) - jnp.sum(lx) * jnp.sum(ly)
            den = n * jnp.sum(lx * lx) - jnp.sum(lx) ** 2
            return jnp.clip(-num / den, 1.0, 2.0)

        def _wave_filter(D, d):
            k = jnp.fft.fftfreq(d).astype(jnp.float32)
            ka = jnp.abs(k) + 1e-08
            omega = 1.0 + 0.2 * D
            a = 1.0 + 0.5 * D
            b = 0.1 * D
            real = jnp.sin(omega * D + a * ka)
            phase = omega * D - ka + b * ka ** 2
            return real * jnp.exp(1j * phase)

        def _golay_correct(bits):
            syn = (bits @ _H.T > 0.5).astype(jnp.float32)
            w = syn.sum(-1)
            _, idx = jax.lax.top_k(syn, 3)
            take = (jnp.arange(3)[None, :] < jnp.minimum(w, 3.0)[:, None]).astype(jnp.float32)
            pattern = (jax.nn.one_hot(idx, 24, dtype=jnp.float32) * take[..., None]).sum(axis=1)
            do_fix = ((w > 0) & (w <= 3))[:, None]
            return jnp.where(do_fix, jnp.mod(bits + pattern, 2.0), bits)
        B, S, E = x.shape
        D = _fractal_dimension(x)
        filt = _wave_filter(D, E)
        x1 = jnp.fft.ifft(jnp.fft.fft(x, axis=-1) * filt, axis=-1).real.astype(x.dtype)
        lat = x1 @ W_el + b_el
        bits = (jax.nn.sigmoid(lat) > 0.5).astype(jnp.float32).reshape(B * S, 24)
        corrected = _golay_correct(bits).reshape(B, S, 24)
        return x1 + corrected @ W_le + b_le

    def _L0_ffn_ref(hidden_states, router_w, e_bias, Wg, Wu, Wd, SWg, SWu, SWd):
        import jax, jax.numpy as jnp
        import numpy as np
        H = 128
        I = 64
        E = 64
        G = 8
        TOPK_GROUP = 4
        K = 8
        I_SH = 128
        SCALE = 2.5

        def _route(x, router_w, e_bias):
            T = x.shape[0]
            scores = jax.nn.sigmoid(x.astype(jnp.float32) @ router_w.T.astype(jnp.float32))
            sfc = jax.lax.stop_gradient(scores) + e_bias[None, :]
            group_scores = jax.lax.top_k(sfc.reshape(T, G, E // G), 2)[0].sum(-1)
            _, gidx = jax.lax.top_k(group_scores, TOPK_GROUP)
            gmask = jax.nn.one_hot(gidx, G, dtype=sfc.dtype).sum(1)
            smask = jnp.repeat(gmask, E // G, axis=1)
            masked = jnp.where(smask > 0, sfc, 0.0)
            _, topk_idx = jax.lax.top_k(masked, K)
            w = jnp.take_along_axis(scores, topk_idx, axis=1)
            w = w / (w.sum(-1, keepdims=True) + 1e-20)
            return (topk_idx, w * SCALE)
        orig_shape = hidden_states.shape
        x = hidden_states.reshape(-1, orig_shape[-1])
        T = x.shape[0]
        topk_idx, topk_w = _route(x, router_w, e_bias)
        coef = jnp.zeros((T, E), topk_w.dtype).at[jnp.arange(T)[:, None], topk_idx].add(topk_w)
        g = jnp.einsum('th,ehi->tei', x, Wg)
        u = jnp.einsum('th,ehi->tei', x, Wu)
        h = jax.nn.silu(g) * u * coef[:, :, None]
        moe_out = jnp.einsum('tei,eih->th', h, Wd)
        shared = jax.nn.silu(x @ SWg) * (x @ SWu) @ SWd
        return (moe_out + shared).reshape(orig_shape)
    x = L0_attn_x
    xn = _layernorm(x, axis=-1)
    s = _L0_attn_ref(xn, L0_attn_W_el, L0_attn_b_el, L0_attn_W_le, L0_attn_b_le)
    g = _silu(_L0_ffn_ref(xn, L0_ffn_router_w, L0_ffn_e_bias, L0_ffn_Wg, L0_ffn_Wu, L0_ffn_Wd, L0_ffn_SWg, L0_ffn_SWu, L0_ffn_SWd))
    x = x + s * g
    return x

_drawn_inputs = setup_inputs


def setup_inputs(seed=0):
    import zlib

    import numpy as np

    out = dict(_drawn_inputs(seed))
    spreads = {'L0_attn_b_el': (0.0, 0.8), 'L0_attn_b_le': (0.0, 0.8), 'L0_ffn_e_bias': (0.0, 0.8)}
    factors = {'L0_attn_W_el': 8.0,
     'L0_attn_W_le': 8.0,
     'L0_ffn_router_w': 8.0,
     'L0_ffn_Wg': 8.0,
     'L0_ffn_Wu': 8.0,
     'L0_ffn_Wd': 8.0,
     'L0_ffn_SWg': 8.0,
     'L0_ffn_SWu': 8.0,
     'L0_ffn_SWd': 8.0}
    for name, (base, spread) in spreads.items():
        noise = np.random.default_rng([zlib.crc32(name.encode()), seed]).standard_normal(out[name].shape)
        drawn = base * np.exp(spread * noise) if base else spread * noise
        out[name] = jnp.asarray(drawn.astype(out[name].dtype))
    for name, factor in factors.items():
        out[name] = (out[name] * factor).astype(out[name].dtype)
    return out
```

```python
from contextlib import ExitStack

import concourse.bass as bass
from concourse import mybir

ALU = mybir.AluOpType
ACT = mybir.ActivationFunctionType
AX = mybir.AxisListType
F32 = mybir.dt.float32
F32R = mybir.dt.float32r
BF16 = mybir.dt.bfloat16
I32 = mybir.dt.int32

P = 128
D = 128
CODE = 24
CHECK = 12
NE = 64
NG = 8
GE = NE // NG
TOPG = 4
DI = 64
PAIR = 2
NPAIR = NE // PAIR
SCALE = 2.5
LN_EPS = 1e-5
FD_EPS = 1e-10
SCALES = (2, 4, 8, 16, 32)
BIG = 3.0e38
SIG_HALF = 2.0 ** -24

C_IDENT = 0
C_DFT = 128
C_HB = 256
C_WB = 384
C_TRI = 512
C_IOTA = 576
C_KA = 640
C_KA2 = 641
C_EIDX = 642
C_ONE = 643
C_LX = 644
NCONST = 652


def recurrent_block_kernel(nc, x, const, w_el, wle_pad, bel_col, router_t, e_bias, wg, wu, wd, shared, out):
    T = x.shape[0]
    NT = T // P
    NCH = 4
    CT = NT // NCH
    QT = NT // 4
    BLK = 512
    TB = BLK // P
    NB = T // BLK
    HALF = T // 2
    HB = HALF // BLK
    ND = 2 * HB

    x_rows = x.rearrange("(p j) e -> p (j e)", j=NT)
    out_rows = out.rearrange("(p j) e -> p (j e)", j=NT)
    coef_dram = nc.dram_tensor("coef_by_expert", [NE, T], F32).ap()

    with ExitStack() as ctx:
        def sb(name, shape, dt=F32):
            return ctx.enter_context(nc.sbuf_tensor(name, shape, dt))

        def sem(name):
            return ctx.enter_context(nc.semaphore(name))

        gu_ps = ctx.enter_context(nc.psum_tensor("gu_ps", [P, 4, BLK], F32))
        y_ps = ctx.enter_context(nc.psum_tensor("y_ps", [P, 4, BLK], F32))

        x_sb = sb("x_sb", [P, NT * D])
        cst = sb("cst", [P, NCONST])
        wel_sb = sb("wel_sb", [P, CODE])
        wle_sb = sb("wle_sb", [P, 4 * D])
        bel_sb = sb("bel_sb", [P, 1])
        rt_sb = sb("rt_sb", [P, NE])
        eb_sb = sb("eb_sb", [P, NE])
        bn6 = sb("bn6", [P, NT, 6])
        mv = sb("mv", [P, NT, 2])
        std = sb("std", [P, NT])
        rstd = sb("rstd", [P, NT])
        xn = sb("xn", [P, NT * D])
        xh = sb("xh", [P, T], F32R)
        xl = sb("xl", [P, T], F32R)
        mm = sb("mm", [P, 2, NCH])
        mm2 = sb("mm2", [P, 2])
        mmr = sb("mmr", [P, 2])
        den = sb("den", [1, 2])
        blk = sb("blk", [1, 1024])
        over = sb("over", [1, 1024])
        sums = sb("sums", [1, 8])
        cnt = sb("cnt", [1, 8])
        dim = sb("dim", [1, 4])
        dimc = sb("dimc", [P, 1])
        ang = sb("ang", [P, 12])
        dft_f = sb("dft_f", [P, D])
        circ = sb("circ", [P, D])
        circ_h = sb("circ_h", [P, D], F32R)
        circ_l = sb("circ_l", [P, D], F32R)
        cel_h = sb("cel_h", [P, 4, D], F32R)
        cel_l = sb("cel_l", [P, 4, D], F32R)
        hb_bf = sb("hb_bf", [P, P], BF16)
        wb_bf = sb("wb_bf", [P, P], BF16)
        bits = sb("bits", [P, 2 * BLK], BF16)
        syn = sb("syn", [P, 2 * BLK], BF16)
        pat = sb("pat", [P, 2 * BLK], BF16)
        corr = sb("corr", [P, 2 * BLK], F32R)
        wle_h = sb("wle_h", [P, 4 * D], F32R)
        wle_l = sb("wle_l", [P, 4 * D], F32R)
        s_sb = sb("s_sb", [P, NT * D])
        rt_h = sb("rt_h", [P, NE], F32R)
        rt_l = sb("rt_l", [P, NE], F32R)
        score = sb("score", [P, NT, NE])
        sfc = sb("sfc", [P, CT, NE])
        hi4 = sb("hi4", [P, CT * NG, 4])
        lo4 = sb("lo4", [P, CT * NG, 4])
        hi2 = sb("hi2", [P, CT * NG, 2])
        lo2 = sb("lo2", [P, CT * NG, 2])
        lo2b = sb("lo2b", [P, CT * NG, 2])
        top1 = sb("top1", [P, CT * NG])
        sec1 = sb("sec1", [P, CT * NG])
        sec2 = sb("sec2", [P, CT * NG])
        gsx = sb("gsx", [P, CT, TOPG + NG])
        gtop = sb("gtop", [P, CT, 8])
        gtaken = sb("gtaken", [P, CT, TOPG + NG])
        gmask = sb("gmask", [P, CT * NG])
        masked = sb("masked", [P, CT, NE])
        etop = sb("etop", [P, CT, 8])
        taken = sb("taken", [P, CT, NE])
        anyc = sb("anyc", [P, NCH, NE])
        used = sb("used", [P, NCH, NE])
        wsel = sb("wsel", [P, CT, NE])
        wsum = sb("wsum", [P, CT])
        winv = sb("winv", [P, CT])
        coef = sb("coef", [P, 2, CT, NE])
        coef_t = sb("coef_t", [P, NCH, BLK])
        act_c = sb("act_c", [NE, 1])
        rk = sb("rk", [NE, 6])
        place = sb("place", [NE, NE])
        order = sb("order", [1, NE + 2 * PAIR], I32)
        nact = sb("nact", [1, 1], I32)
        WP = 3 * D
        raw = sb("raw", [P, WP])
        sraw = sb("sraw", [P, WP])
        sw_h = sb("sw_h", [P, WP], F32R)
        sw_l = sb("sw_l", [P, WP], F32R)
        w_h = [sb(f"w_h{b}", [P, WP], F32R) for b in range(2)]
        w_l = [sb(f"w_l{b}", [P, WP], F32R) for b in range(2)]
        cb = [sb(f"cb{b}", [P, HALF]) for b in range(2)]
        ones = sb("ones", [P, BLK])
        sg = [sb(f"sg{b}", [P, BLK]) for b in range(2)]
        mt = [sb(f"mt{b}", [P, BLK]) for b in range(2)]
        ht = [sb(f"ht{b}", [P, BLK]) for b in range(2)]
        hh = [sb(f"hh{b}", [P, BLK], F32R) for b in range(2)]
        hl = [sb(f"hl{b}", [P, BLK], F32R) for b in range(2)]
        res = xn[:, 0:HALF]
        gt = xn[:, HALF:T].rearrange("p (b n) -> p b n", n=BLK)

        ident = cst[:, C_IDENT:C_IDENT + P]
        dft = cst[:, C_DFT:C_DFT + D]

        x_in = [sem(f"x_in{c}") for c in range(NCH)]
        cst_in = sem("cst_in")
        small_in = sem("small_in")
        dve_step = sem("dve_step")
        act_step = sem("act_step")
        pool_step = sem("pool_step")
        var_ready = sem("var_ready")
        std_ready = sem("std_ready")
        xn_ready = sem("xn_ready")
        xt_ready = sem("xt_ready")
        xh_ready = sem("xh_ready")
        xl_ready = sem("xl_ready")
        rt_h_ready = sem("rt_h_ready")
        rt_l_ready = sem("rt_l_ready")
        logit_ready = sem("logit_ready")
        score_ready = sem("score_ready")
        mm_ready = sem("mm_ready")
        mmr_ready = sem("mmr_ready")
        cnt_ready = sem("cnt_ready")
        ln_ready = sem("ln_ready")
        dim_ready = sem("dim_ready")
        dimb_ready = sem("dimb_ready")
        ang_ready = sem("ang_ready")
        sin_ready = sem("sin_ready")
        dftf_ready = sem("dftf_ready")
        circ_ps_ready = sem("circ_ps_ready")
        circ_ready = sem("circ_ready")
        circ_h_ready = sem("circ_h_ready")
        circ_l_ready = sem("circ_l_ready")
        cel_ps_ready = sem("cel_ps_ready")
        cel_h_ready = sem("cel_h_ready")
        cel_l_ready = sem("cel_l_ready")
        zero_ready = sem("zero_ready")
        hbwb_ready = sem("hbwb_ready")
        wle_h_ready = sem("wle_h_ready")
        wle_l_ready = sem("wle_l_ready")
        lat_ready = sem("lat_ready")
        bits_ready = sem("bits_ready")
        syn_ps_ready = sem("syn_ps_ready")
        syn_ready = sem("syn_ready")
        wt_ps_ready = sem("wt_ps_ready")
        corr_ready = sem("corr_ready")
        s_ps_ready = sem("s_ps_ready")
        s_ready = sem("s_ready")
        coef_ready = sem("coef_ready")
        coeft_ps_ready = sem("coeft_ps_ready")
        coeft_ready = sem("coeft_ready")
        coeft_out = [sem(f"coeft_out{c}") for c in range(NCH)]
        used_ready = sem("used_ready")
        used_ps_ready = sem("used_ps_ready")
        active_ready = sem("active_ready")
        rank_ps_ready = sem("rank_ps_ready")
        place_ready = sem("place_ready")
        order_ps_ready = sem("order_ps_ready")
        order_ready = sem("order_ready")
        sw_h_ready = sem("sw_h_ready")
        sw_l_ready = sem("sw_l_ready")
        H = []
        for h in range(2):
            H.append({n: sem(f"{n}_{h}") for n in (
                "raw_in", "cb_in0", "cb_in1", "w_h_ready", "w_l_ready", "g_ready", "u_ready", "silu_ready",
                "m_ready", "h_ready", "hh_ready", "hl_ready", "down_done", "gt_ready", "gback_ready",
                "gs_ready", "res_ready", "res_out")})

        block = ctx.enter_context(nc.Block())

        def tile(buf, j):
            return buf[:, j * D:(j + 1) * D]

        def blocks_of(h, b):
            return slice(h * HALF + b * BLK, h * HALF + (b + 1) * BLK)

        def pairs(n_active):
            return (n_active + 1) // 2

        @block.sync
        def _(sp):
            sp.dma_start(cst[:, :], const).then_inc(cst_in, 16)
            w = CT * D
            for c in range(NCH):
                sp.dma_start(x_sb[:, c * w:(c + 1) * w], x_rows[:, c * w:(c + 1) * w]).then_inc(x_in[c], 16)
            for dst, src in ((rt_sb, router_t), (wel_sb, w_el), (wle_sb, wle_pad), (bel_sb, bel_col), (sraw, shared)):
                sp.dma_start(dst[:, :], src).then_inc(small_in, 16)
            sp.dma_start(eb_sb[:, :], e_bias.to_broadcast([P, NE])).then_inc(small_in, 16)
            by_tile = coef_dram.rearrange("e (c t a p) -> e c t a p", c=NCH, a=2, p=P)
            for c in range(NCH):
                sp.wait_ge(coeft_ready, c + 1)
                for a in range(2):
                    sp.dma_start(by_tile[:, c, :, a, :],
                                 coef_t[a * NE:(a + 1) * NE, c, :].rearrange("e (t p) -> e t p", p=P)
                                 ).then_inc(coeft_out[c], 16)
            for c in range(NCH):
                sp.wait_ge(coeft_out[c], 32)
            sp.wait_ge(order_ready, 3)
            n_pairs = pairs(sp.value_load(nact[0:1, 0:1], min_val=1, max_val=NE))

            def experts(k):
                return [sp.value_load(order[0:1, bass.ds(PAIR * (k - 1) + m, 1)], min_val=0, max_val=NE - 1)
                        for m in range(PAIR)]

            def load_pair(h, chosen, b):
                s = H[h]
                for m, e in enumerate(chosen):
                    pick = bass.ds(e, 1)
                    sp.dma_start(raw[:, m * DI:(m + 1) * DI],
                                 wg[pick].rearrange("a h i -> (a h) i")).then_inc(s["raw_in"], 16)
                    sp.dma_start(raw[:, D + m * DI:D + (m + 1) * DI],
                                 wu[pick].rearrange("a h i -> (a h) i")).then_inc(s["raw_in"], 16)
                    sp.dma_start(raw[m * DI:(m + 1) * DI, 2 * D:3 * D],
                                 wd[pick].rearrange("a i h -> (a i) h")).then_inc(s["raw_in"], 16)
                    sp.dma_start(cb[b][m * DI:(m + 1) * DI, :],
                                 coef_dram[pick, h * HALF:(h + 1) * HALF].to_broadcast([DI, HALF])
                                 ).then_inc(s[f"cb_in{b}"], 16)

            for h in range(2):
                s = H[h]
                chosen = experts(1)
                if h == 1:
                    o = H[0]
                    sp.wait_ge(o["h_ready"], (n_pairs + 1) * HB)
                    sp.wait_ge(o["w_l_ready"], n_pairs + 1)
                    sp.wait_ge(o["cb_in0"], (n_pairs + 2) // 2 * 32)
                    sp.wait_ge(o["cb_in1"], (n_pairs + 1) // 2 * 32)
                load_pair(h, chosen, 0)

                def load_next(k, b):
                    chosen = experts(k + 1)
                    sp.wait_ge(s["h_ready"], k * HB)
                    sp.wait_ge(s["w_l_ready"], k)
                    load_pair(h, chosen, b)

                load_next(1, 1)
                with sp.Fori(0, NPAIR // 2) as i:
                    for b in range(2):
                        k = i * 2 + (b + 2)
                        with sp.If(k <= n_pairs):
                            load_next(k, b)
                for g in range(HB):
                    sp.wait_ge(s["res_ready"], g + 1)
                    at = slice((h * HALF // BLK + g) * BLK, (h * HALF // BLK + g + 1) * BLK)
                    sp.dma_start(out_rows[:, at], res[:, g * BLK:(g + 1) * BLK]).then_inc(s["res_out"], 16)
            for h in range(2):
                sp.wait_ge(H[h]["res_out"], 16 * HB)

        @block.tensor
        def _(pe):
            def mm3(out_ap, lhs, rhs, start=True):
                (lh, ll), (rh, rl) = lhs, rhs
                pe.matmul(out_ap, ll, rh, start=start, stop=False, skip_group_check=True)
                pe.matmul(out_ap, lh, rl, start=False, stop=False, skip_group_check=True)
                return pe.matmul(out_ap, lh, rh, start=False, stop=True, skip_group_check=True)

            pe.wait_ge(cst_in, 16)

            def transposes(g):
                pe.wait_ge(xn_ready, g // 2 + 1)
                if g >= 4:
                    pe.wait_ge(xl_ready, g - 3)
                for t in range(TB):
                    last = pe.transpose(gu_ps[:, g % 4, t * P:(t + 1) * P], tile(xn, g * TB + t), ident)
                last.then_inc(xt_ready, 1)

            def logits(g):
                pe.wait_ge(xl_ready, g + 1)
                if g == 0:
                    pe.wait_ge(rt_l_ready, 1)
                for t in range(TB):
                    j = g * TB + t
                    at = j % CT * NE
                    last = mm3(y_ps[:, j // CT, at:at + NE], (tile(xh, j), tile(xl, j)), (rt_h[:, :], rt_l[:, :]))
                last.then_inc(logit_ready, 1)

            for g in range(NB + 1):
                if g < NB:
                    transposes(g)
                if g >= 1:
                    logits(g - 1)

            misc = gu_ps[:, 3, :]
            pe.wait_ge(xl_ready, NB)
            pe.wait_ge(dim_ready, 1)
            pe.matmul(misc[:, 0:1], cst[0:1, C_ONE:C_ONE + 1].to_broadcast([1, P]), dim[0:1, 3:4], start=True, stop=True).then_inc(dimb_ready, 1)
            pe.wait_ge(dftf_ready, 1)
            pe.matmul(misc[:, 128:256], dft_f[:, :], dft, start=True, stop=True).then_inc(circ_ps_ready, 1)
            pe.wait_ge(circ_ready, 1)
            pe.matmul(misc[:, 256:256 + CODE], circ[:, :], wel_sb[:, :], start=True, stop=True).then_inc(cel_ps_ready, 1)
            pe.wait_ge(cel_l_ready, 1)
            for c in range(2):
                for q in range(4):
                    at = slice(q * QT * P + c * BLK, q * QT * P + (c + 1) * BLK)
                    o = gu_ps[:, c, :]
                    pe.matmul(o, cel_l[:, q, :], xh[:, at], start=(q == 0), stop=False)
                    pe.matmul(o, cel_h[:, q, :], xl[:, at], start=False, stop=False)
                    last = pe.matmul(o, cel_h[:, q, :], xh[:, at], start=False, stop=(q == 3))
                last.then_inc(lat_ready, 1)
            pe.wait_ge(hbwb_ready, 2)
            for c in range(2):
                pe.wait_ge(bits_ready, c + 1)
                pe.matmul(gu_ps[:, 2 + c, :], hb_bf[:, :], bits[:, c * BLK:(c + 1) * BLK],
                          start=True, stop=True).then_inc(syn_ps_ready, 1)
            for c in range(2):
                pe.wait_ge(syn_ready, c + 1)
                pe.matmul(gu_ps[:, c, :], wb_bf[:, :], syn[:, c * BLK:(c + 1) * BLK],
                          start=True, stop=True).then_inc(wt_ps_ready, 1)
            pe.wait_ge(circ_l_ready, 1)
            pe.wait_ge(wle_l_ready, 1)
            pe.wait_ge(corr_ready, 2)
            for g in range(NB):
                if g >= 4:
                    pe.wait_ge(s_ready, g - 3)
                for t in range(TB):
                    j = g * TB + t
                    q, c = divmod(j, QT)
                    o = gu_ps[:, g % 4, t * D:(t + 1) * D]
                    mm3(o, (tile(xh, j), tile(xl, j)), (circ_h[:, :], circ_l[:, :]))
                    cc = corr[:, c * P:(c + 1) * P]
                    pe.matmul(o, cc, wle_l[:, q * D:(q + 1) * D], start=False, stop=False, skip_group_check=True)
                    last = pe.matmul(o, cc, wle_h[:, q * D:(q + 1) * D], start=False, stop=True,
                                     skip_group_check=True)
                last.then_inc(s_ps_ready, 1)
            for c in range(NCH):
                pe.wait_ge(coef_ready, c + 1)
                pe.wait_ge(score_ready, c + 1)
                for t in range(CT // 2):
                    last = pe.transpose(y_ps[:, c, t * P:(t + 1) * P],
                                        coef[:, c % 2, 2 * t:2 * t + 2, :].rearrange("p t e -> p (t e)"), ident)
                last.then_inc(coeft_ps_ready, 1)
            pe.wait_ge(s_ready, NB)
            pe.wait_ge(used_ready, 1)
            for c in range(NCH):
                last = pe.matmul(misc[0:NE, 0:1], used[:, c, :], cst[:, C_ONE:C_ONE + 1], start=(c == 0),
                                 stop=(c == NCH - 1))
            last.then_inc(used_ps_ready, 1)
            pe.wait_ge(active_ready, 1)
            pe.matmul(misc[0:NE, 8:9], cst[0:NE, C_TRI:C_TRI + NE], act_c[:, :], start=True, stop=True)
            pe.matmul(misc[0:NE, 9:10], cst[0:NE, C_ONE:C_ONE + 1].to_broadcast([NE, NE]), act_c[:, :],
                      start=True, stop=True).then_inc(rank_ps_ready, 1)
            pe.wait_ge(place_ready, 1)
            pe.matmul(misc[0:1, 64:64 + NE], cst[0:NE, C_EIDX:C_EIDX + 1], place[:, :],
                      start=True, stop=True).then_inc(order_ps_ready, 1)

            pe.wait_ge(order_ready, 3)
            pe.wait_ge(coeft_ready, NCH)
            pe.wait_ge(sw_l_ready, 1)
            n_pairs = pairs(pe.value_load(nact[0:1, 0:1], min_val=1, max_val=NE))
            S = (sw_h, sw_l)
            W = [(w_h[b], w_l[b]) for b in range(2)]

            def down(h, n, b, w, first):
                s = H[h]
                pe.wait_ge(s["hl_ready"], n + 1)
                wh, wl = (v[:, 2 * D:3 * D] for v in w)
                mm3(y_ps[:, b, :], (wh, wl), (hh[b % 2][:, :], hl[b % 2][:, :]),
                    start=first).then_inc(s["down_done"], 1)

            def pair(h, k, w, before):
                s = H[h]
                for b in range(HB):
                    n = k * HB + b
                    if not isinstance(n, int) or n >= 2:
                        pe.wait_ge(s["m_ready"], n - 1)
                    at = blocks_of(h, b)
                    for what, name in ((0, "g_ready"), (1, "u_ready")):
                        wh, wl = (v[:, what * D:(what + 1) * D] for v in w)
                        mm3(gu_ps[:, 2 * (b % 2) + what, :], (wh, wl), (xh[:, at], xl[:, at])).then_inc(s[name], 1)
                    if b >= 2:
                        down(h, n - 2, b - 2, w, before is None)
                    elif before is not None:
                        down(h, n - 2, b + 2, before, before is S)

            for h in range(2):
                s = H[h]
                if h == 1:
                    pe.wait_ge(H[0]["gs_ready"], HB)
                pair(h, 0, S, None)
                pe.wait_ge(s["w_l_ready"], 1)
                pair(h, 1, W[0], S)
                with pe.Fori(0, NPAIR // 2) as i:
                    for b in range(2):
                        k = i * 2 + (b + 2)
                        with pe.If(k <= n_pairs):
                            pe.wait_ge(s["w_l_ready"], k)
                            pair(h, k, W[1 - b], W[b])
                last_n = n_pairs * HB
                with pe.If((n_pairs % 2) > 0):
                    down(h, last_n + 2, 2, W[0], False)
                    down(h, last_n + 3, 3, W[0], False)
                with pe.Else():
                    down(h, last_n + 2, 2, W[1], False)
                    down(h, last_n + 3, 3, W[1], False)
                for g in range(HB):
                    pe.wait_ge(s["gt_ready"], g + 1)
                    for t in range(TB):
                        last = pe.transpose(gu_ps[:, g, t * P:(t + 1) * P], gt[:, g, t * P:(t + 1) * P], ident)
                    last.then_inc(s["gback_ready"], 1)

        @block.scalar
        def _(act):
            def chain(ins, count):
                ins.then_inc(act_step, 1)
                act.wait_ge(act_step, count)

            act.wait_ge(small_in, 96)
            act.activation(rt_h[:, :], rt_sb[:, :], ACT.Copy).then_inc(rt_h_ready, 1)
            act.activation(sw_h[:, :], sraw[:, :], ACT.Copy).then_inc(sw_h_ready, 1)
            act.activation(wle_h[:, :], wle_sb[:, :], ACT.Copy).then_inc(wle_h_ready, 1)
            for c in range(NCH):
                act.wait_ge(var_ready, c + 1)
                act.activation(std[:, c * CT:(c + 1) * CT], mv[:, c * CT:(c + 1) * CT, 1], ACT.Sqrt,
                               ).then_inc(std_ready, 1)
            for g in range(NB):
                act.wait_ge(xt_ready, g + 1)
                act.activation(xh[:, g * BLK:(g + 1) * BLK], gu_ps[:, g % 4, :], ACT.Copy).then_inc(xh_ready, 1)
            for c in range(NCH):
                act.wait_ge(logit_ready, 2 * c + 2)
                act.activation(score[:, c * CT:(c + 1) * CT, :].rearrange("p t e -> p (t e)"), y_ps[:, c, :],
                               ACT.Sigmoid).then_inc(score_ready, 1)
            act.wait_ge(cnt_ready, 1)
            act.activation(cnt[0:1, 0:5], sums[0:1, 0:5], ACT.Ln).then_inc(ln_ready, 1)
            act.wait_ge(ang_ready, 1)
            act.activation(ang[:, 6:8], ang[:, 4:6], ACT.Sin).then_inc(sin_ready, 1)
            act.wait_ge(circ_ps_ready, 1)
            act.activation(circ[:, :], gu_ps[:, 3, 128:256], ACT.Copy).then_inc(circ_ready, 1)
            act.wait_ge(circ_ready, 1)
            act.activation(circ_h[:, :], circ[:, :], ACT.Copy).then_inc(circ_h_ready, 1)
            act.wait_ge(cel_ps_ready, 1)
            act.wait_ge(zero_ready, 1)
            for q in range(4):
                last = act.activation(cel_h[:, q, 32 * q:32 * q + CODE], gu_ps[:, 3, 256:256 + CODE], ACT.Copy)
            last.then_inc(cel_h_ready, 1)
            for g in range(NB):
                act.wait_ge(s_ps_ready, g + 1)
                act.activation(s_sb[:, g * BLK:(g + 1) * BLK], gu_ps[:, g % 4, :], ACT.Copy).then_inc(s_ready, 1)
            for c in range(NCH):
                act.wait_ge(coeft_ps_ready, c + 1)
                act.activation(coef_t[:, c, :], y_ps[:, c, :], ACT.Copy).then_inc(coeft_ready, 1)

            act.wait_ge(order_ready, 3)
            n_pairs = pairs(act.value_load(nact[0:1, 0:1], min_val=1, max_val=NE))

            def split_high(h, k, b):
                s = H[h]
                act.wait_ge(s["raw_in"], 96 * k)
                act.activation(w_h[b][:, :], raw[:, :], ACT.Copy).then_inc(s["w_h_ready"], 1)

            def high(h, n, b):
                s = H[h]
                act.wait_ge(s["h_ready"], n + 1)
                if not isinstance(n, int) or n >= 2:
                    act.wait_ge(s["down_done"], n - 1)
                act.activation(hh[b % 2][:, :], ht[b % 2][:, :], ACT.Copy).then_inc(s["hh_ready"], 1)

            def pair(h, k, nxt):
                s = H[h]
                for b in range(HB):
                    n = k * HB + b
                    act.wait_ge(s["g_ready"], n + 1)
                    act.activation(sg[b % 2][:, :], gu_ps[:, 2 * (b % 2), :], ACT.Silu).then_inc(s["silu_ready"], 1)
                    if not isinstance(n, int) or n >= 1:
                        high(h, n - 1, (b - 1) % HB)
                    if b == 2:
                        if not isinstance(k, int) or k >= 2:
                            act.wait_ge(s["down_done"], k * HB)
                        split_high(h, k + 1, nxt)

            for h in range(2):
                s = H[h]
                pair(h, 0, 0)
                pair(h, 1, 1)
                with act.Fori(0, NPAIR // 2) as i:
                    for b in range(2):
                        k = i * 2 + (b + 2)
                        with act.If(k <= n_pairs):
                            pair(h, k, b)
                high(h, n_pairs * HB + (HB - 1), HB - 1)
                act.wait_ge(s["down_done"], (n_pairs + 1) * HB)
                for g in range(HB):
                    act.activation(gt[:, g, :], y_ps[:, g, :], ACT.Silu).then_inc(s["gt_ready"], 1)

        @block.vector
        def _(dve):
            steps = [0]

            def then(ins):
                steps[0] += 1
                ins.then_inc(dve_step, 1)
                dve.wait_ge(dve_step, steps[0])

            dve.memset(cel_h[:, :, :].rearrange("p q c -> p (q c)").bitcast(F32), 0.0)
            dve.memset(order[:, :], 0)
            then(dve.memset(cel_l[:, :, :].rearrange("p q c -> p (q c)").bitcast(F32), 0.0))
            dve.memset(gsx[:, :, :], BIG).then_inc(zero_ready, 1)
            dve.wait_ge(cst_in, 16)
            for c in range(NCH):
                dve.wait_ge(x_in[c], 16)
                tiles = range(c * CT, (c + 1) * CT)
                cs = slice(c * CT, (c + 1) * CT)
                for j in tiles:
                    last = dve.bn_stats(bn6[:, j, :], tile(x_sb, j))
                then(last)
                for j in tiles:
                    last = dve.bn_aggr(mv[:, j, :], bn6[:, j, :])
                then(last)
                then(dve.tensor_scalar(mv[:, cs, 1], mv[:, cs, 1], LN_EPS, None, ALU.add))
                dve.tensor_copy(rstd[:, cs], mv[:, cs, 1]).then_inc(var_ready, 1)
                dve.wait_ge(std_ready, c + 1)
                then(dve.reciprocal(rstd[:, cs], std[:, cs]))
                then(dve.tensor_tensor(std[:, cs], rstd[:, cs], rstd[:, cs], ALU.mult))
                then(dve.tensor_tensor(std[:, cs], std[:, cs], mv[:, cs, 1], ALU.mult))
                then(dve.tensor_scalar(std[:, cs], std[:, cs], -0.5, 1.5, ALU.mult, ALU.add))
                then(dve.tensor_tensor(rstd[:, cs], rstd[:, cs], std[:, cs], ALU.mult))
                for j in tiles:
                    last = dve.tensor_scalar(tile(xn, j), tile(x_sb, j), mv[:, j, 0:1], rstd[:, j:j + 1],
                                             ALU.subtract, ALU.mult)
                last.then_inc(xn_ready, 1)
                if c == 0:
                    dve.wait_ge(rt_h_ready, 1)
                    dve.tensor_tensor(rt_l[:, :], rt_sb[:, :], rt_h[:, :].bitcast(F32), ALU.subtract)\
                       .then_inc(rt_l_ready, 1)
                dve.wait_ge(xn_ready, c + 1)
                w = slice(c * CT * D, (c + 1) * CT * D)
                dve.tensor_reduce(mm[:, 0, c:c + 1], xn[:, w], AX.X, ALU.max)
                last = dve.tensor_reduce(mm[:, 1, c:c + 1], xn[:, w], AX.X, ALU.min)
            then(last)
            then(dve.tensor_reduce(mm2[:, 0:1], mm[:, 0, :], AX.X, ALU.max))
            then(dve.tensor_reduce(mm2[:, 1:2], mm[:, 1, :], AX.X, ALU.min))
            dve.tensor_scalar(mm2[:, 1:2], mm2[:, 1:2], -1.0, None, ALU.mult).then_inc(mm_ready, 1)
            for g in range(NB):
                dve.wait_ge(xh_ready, g + 1)
                at = slice(g * BLK, (g + 1) * BLK)
                dve.tensor_tensor(xl[:, at], gu_ps[:, g % 4, :], xh[:, at].bitcast(F32), ALU.subtract)\
                   .then_inc(xl_ready, 1)
            dve.wait_ge(mmr_ready, 1)
            then(dve.tensor_scalar(den[0:1, 0:1], mmr[0:1, 0:1], mmr[0:1, 1:2], FD_EPS, ALU.add, ALU.add))
            then(dve.reciprocal(den[0:1, 1:2], den[0:1, 0:1]))
            then(dve.tensor_scalar(blk[:, :], xn[0:1, 0:1024], mmr[0:1, 1:2], den[0:1, 1:2], ALU.add, ALU.mult))
            for i, sc in enumerate(SCALES):
                last = dve.tensor_reduce(sums[0:1, i:i + 1], blk[0:1, 0:sc * sc], AX.X, ALU.add)
            then(last)
            for i, sc in enumerate(SCALES):
                last = dve.tensor_scalar(cnt[0:1, i:i + 1], sums[0:1, i:i + 1], 1.0 / (sc * sc), None, ALU.mult)
            then(last)
            for i, sc in enumerate(SCALES):
                then(dve.tensor_scalar(over[0:1, 0:sc * sc], blk[0:1, 0:sc * sc], cnt[0:1, i:i + 1], None, ALU.is_gt))
                then(dve.tensor_reduce(sums[0:1, i:i + 1], over[0:1, 0:sc * sc], AX.X, ALU.add))
            dve.tensor_scalar(sums[0:1, 0:5], sums[0:1, 0:5], 1.0, None, ALU.max).then_inc(cnt_ready, 1)
            dve.wait_ge(ln_ready, 1)
            then(dve.tensor_tensor(sums[0:1, 0:5], cnt[0:1, 0:5], cst[0:1, C_LX:C_LX + 5], ALU.mult))
            then(dve.tensor_reduce(dim[0:1, 0:1], sums[0:1, 0:5], AX.X, ALU.add))
            dve.tensor_scalar(dim[0:1, 3:4], dim[0:1, 0:1], 1.0, 2.0, ALU.max, ALU.min).then_inc(dim_ready, 1)
            dve.wait_ge(dimb_ready, 1)
            then(dve.tensor_copy(dimc[:, :], gu_ps[:, 3, 0:1]))
            dcol, ka, ka2 = dimc[:, 0:1], cst[:, C_KA:C_KA + 1], cst[:, C_KA2:C_KA2 + 1]
            dve.tensor_scalar(ang[:, 0:1], dcol, 0.2, 1.0, ALU.mult, ALU.add)
            dve.tensor_scalar(ang[:, 1:2], dcol, 0.5, 1.0, ALU.mult, ALU.add)
            then(dve.tensor_scalar(ang[:, 2:3], dcol, 0.1, None, ALU.mult))
            dve.tensor_tensor(ang[:, 0:1], ang[:, 0:1], dcol, ALU.mult)
            dve.tensor_tensor(ang[:, 1:2], ang[:, 1:2], ka, ALU.mult)
            then(dve.tensor_tensor(ang[:, 3:4], ang[:, 2:3], ka2, ALU.mult))
            dve.tensor_tensor(ang[:, 8:9], ang[:, 0:1], ang[:, 1:2], ALU.add)
            then(dve.tensor_tensor(ang[:, 9:10], ang[:, 0:1], ka, ALU.subtract))
            then(dve.tensor_tensor(ang[:, 10:11], ang[:, 9:10], ang[:, 3:4], ALU.add))
            dve.tensor_scalar(ang[:, 4:5], ang[:, 8:9], -1.0, 3.14159265358979, ALU.mult, ALU.add)
            dve.tensor_scalar(ang[:, 5:6], ang[:, 10:11], -1.0, 1.5707963267949, ALU.mult, ALU.add)\
               .then_inc(ang_ready, 1)
            dve.wait_ge(sin_ready, 1)
            dve.tensor_scalar(dft_f[:, :], dft, ang[:, 6:7], ang[:, 7:8], ALU.mult, ALU.mult).then_inc(dftf_ready, 1)
            dve.wait_ge(small_in, 96)
            dve.tensor_copy(hb_bf[:, :], cst[:, C_HB:C_HB + P]).then_inc(hbwb_ready, 1)
            dve.tensor_copy(wb_bf[:, :], cst[:, C_WB:C_WB + P]).then_inc(hbwb_ready, 1)
            dve.wait_ge(wle_h_ready, 1)
            dve.tensor_tensor(wle_l[:, :], wle_sb[:, :], wle_h[:, :].bitcast(F32), ALU.subtract).then_inc(wle_l_ready, 1)
            dve.wait_ge(sw_h_ready, 1)
            dve.tensor_tensor(sw_l[:, :], sraw[:, :], sw_h[:, :].bitcast(F32), ALU.subtract).then_inc(sw_l_ready, 1)
            dve.wait_ge(circ_h_ready, 1)
            dve.tensor_tensor(circ_l[:, :], circ[:, :], circ_h[:, :].bitcast(F32), ALU.subtract).then_inc(circ_l_ready, 1)
            dve.wait_ge(cel_h_ready, 1)
            for q in range(4):
                at = slice(32 * q, 32 * q + CODE)
                last = dve.tensor_tensor(cel_l[:, q, at], gu_ps[:, 3, 256:256 + CODE], cel_h[:, q, at].bitcast(F32),
                                         ALU.subtract)
            last.then_inc(cel_l_ready, 1)
            for c in range(2):
                dve.wait_ge(lat_ready, c + 1)
                dve.tensor_scalar(bits[:, c * BLK:(c + 1) * BLK], gu_ps[:, c, :], bel_sb[:, 0:1], SIG_HALF,
                                  ALU.add, ALU.is_gt).then_inc(bits_ready, 1)
            for c in range(2):
                dve.wait_ge(syn_ps_ready, c + 1)
                dve.tensor_scalar(syn[:, c * BLK:(c + 1) * BLK], gu_ps[:, 2 + c, :], 0.5, None, ALU.is_gt)\
                   .then_inc(syn_ready, 1)
            for c in range(2):
                at = slice(c * BLK, (c + 1) * BLK)
                dve.wait_ge(wt_ps_ready, c + 1)
                then(dve.scalar_tensor_tensor(pat[:, at], gu_ps[:, c, :], 3.5, syn[:, at], ALU.is_le, ALU.mult))
                dve.tensor_tensor(corr[:, at], bits[:, at], pat[:, at], ALU.not_equal).then_inc(corr_ready, 1)

            for c in range(NCH):
                sc = score[:, c * CT:(c + 1) * CT, :]
                dve.wait_ge(score_ready, c + 1)
                then(dve.tensor_tensor(sfc[:, :, :], sc, eb_sb[:, :].unsqueeze(1).to_broadcast([P, CT, NE]), ALU.add))
                v = sfc[:, :, :].rearrange("p t (g e) -> p (t g) e", g=NG)
                dve.tensor_tensor(hi4[:, :, :], v[:, :, 0:4], v[:, :, 4:8], ALU.max)
                then(dve.tensor_tensor(lo4[:, :, :], v[:, :, 0:4], v[:, :, 4:8], ALU.min))
                dve.tensor_tensor(hi2[:, :, :], hi4[:, :, 0:2], hi4[:, :, 2:4], ALU.max)
                dve.tensor_tensor(lo2[:, :, :], hi4[:, :, 0:2], hi4[:, :, 2:4], ALU.min)
                then(dve.tensor_tensor(lo2b[:, :, :], lo4[:, :, 0:2], lo4[:, :, 2:4], ALU.max))
                then(dve.tensor_tensor(lo2[:, :, :], lo2[:, :, :], lo2b[:, :, :], ALU.max))
                dve.tensor_tensor(top1[:, :], hi2[:, :, 0], hi2[:, :, 1], ALU.max)
                dve.tensor_tensor(sec1[:, :], hi2[:, :, 0], hi2[:, :, 1], ALU.min)
                then(dve.tensor_tensor(sec2[:, :], lo2[:, :, 0], lo2[:, :, 1], ALU.max))
                then(dve.tensor_tensor(sec1[:, :], sec1[:, :], sec2[:, :], ALU.max))
                then(dve.tensor_tensor(gsx[:, :, TOPG:], top1[:, :].rearrange("p (t g) -> p t g", g=NG),
                                       sec1[:, :].rearrange("p (t g) -> p t g", g=NG), ALU.add))
                for t in range(CT):
                    last = dve.max(gtop[:, t, :], gsx[:, t, :])
                then(last)
                for t in range(CT):
                    last = dve.match_replace(gtaken[:, t, :], gtop[:, t, :], gsx[:, t, :], -BIG)
                then(last)
                then(dve.tensor_scalar(gmask[:, :].rearrange("p (t g) -> p t g", g=NG), gtaken[:, :, TOPG:], -BIG, None,
                                       ALU.is_equal))
                then(dve.tensor_tensor(masked[:, :, :].rearrange("p t (g e) -> p (t g) e", g=NG), v,
                                       gmask[:, :].unsqueeze(2).to_broadcast([P, CT * NG, GE]), ALU.mult))
                for t in range(CT):
                    last = dve.max(etop[:, t, :], masked[:, t, :])
                then(last)
                for t in range(CT):
                    last = dve.match_replace(taken[:, t, :], etop[:, t, :], masked[:, t, :], -BIG)
                then(last)
                dve.tensor_reduce(anyc[:, c, :], taken[:, :, :].rearrange("p t e -> p e t"), AX.X, ALU.min)
                then(dve.scalar_tensor_tensor(wsel[:, :, :], taken[:, :, :], -BIG, sc, ALU.is_equal, ALU.mult))
                then(dve.tensor_reduce(wsum[:, :], wsel[:, :, :], AX.X, ALU.add))
                then(dve.tensor_scalar(wsum[:, :], wsum[:, :], 1e-20, None, ALU.add))
                then(dve.reciprocal(winv[:, :], wsum[:, :]))
                then(dve.tensor_scalar(winv[:, :], winv[:, :], SCALE, None, ALU.mult))
                if c >= 2:
                    dve.wait_ge(coeft_ps_ready, c - 1)
                dve.tensor_tensor(coef[:, c % 2, :, :], wsel[:, :, :],
                                  winv[:, :].unsqueeze(2).to_broadcast([P, CT, NE]), ALU.mult).then_inc(coef_ready, 1)
            dve.tensor_scalar(used[:, :, :], anyc[:, :, :], -BIG, None, ALU.is_equal).then_inc(used_ready, 1)
            misc = gu_ps[:, 3, :]
            dve.wait_ge(used_ps_ready, 1)
            dve.tensor_scalar(act_c[:, :], misc[0:NE, 0:1], 0.5, None, ALU.is_gt).then_inc(active_ready, 1)
            dve.wait_ge(rank_ps_ready, 1)
            then(dve.tensor_copy(rk[:, 0:2], misc[0:NE, 8:10]))
            then(dve.tensor_tensor(rk[:, 2:3], rk[:, 1:2], rk[:, 0:1], ALU.subtract))
            then(dve.tensor_tensor(rk[:, 2:3], rk[:, 2:3], cst[0:NE, C_EIDX:C_EIDX + 1], ALU.add))
            then(dve.tensor_tensor(rk[:, 3:4], rk[:, 0:1], rk[:, 2:3], ALU.subtract))
            then(dve.tensor_tensor(rk[:, 3:4], rk[:, 3:4], act_c[:, :], ALU.mult))
            then(dve.tensor_tensor(rk[:, 4:5], rk[:, 3:4], rk[:, 2:3], ALU.add))
            dve.tensor_scalar(place[:, :], cst[0:NE, C_IOTA:C_IOTA + NE], rk[:, 4:5], None, ALU.is_equal)\
               .then_inc(place_ready, 1)
            dve.tensor_copy(nact[:, :], rk[0:1, 1:2]).then_inc(order_ready, 1)
            dve.wait_ge(order_ps_ready, 1)
            dve.tensor_copy(order[0:1, 0:NE], misc[0:1, 64:64 + NE]).then_inc(order_ready, 1)
            dve.wait_ge(order_ready, 2)
            dve.tensor_copy(dim[0:1, 1:2], dim[0:1, 0:1]).then_inc(order_ready, 1)

            dve.wait_ge(order_ready, 3)
            n_pairs = pairs(dve.value_load(nact[0:1, 0:1], min_val=1, max_val=NE))

            def split_low(h, k, b):
                s = H[h]
                dve.wait_ge(s["w_h_ready"], k)
                dve.tensor_tensor(w_l[b][:, :], raw[:, :], w_h[b][:, :].bitcast(F32), ALU.subtract)\
                   .then_inc(s["w_l_ready"], 1)

            def low(h, n, b):
                s = H[h]
                dve.wait_ge(s["hh_ready"], n + 1)
                dve.tensor_tensor(hl[b % 2][:, :], ht[b % 2][:, :], hh[b % 2][:, :].bitcast(F32), ALU.subtract)\
                   .then_inc(s["hl_ready"], 1)

            def pair(h, k, nxt):
                s = H[h]
                for b in range(HB):
                    n = k * HB + b
                    dve.wait_ge(s["silu_ready"], n + 1)
                    dve.wait_ge(s["u_ready"], n + 1)
                    if not isinstance(n, int) or n >= 2:
                        dve.wait_ge(s["h_ready"], n - 1)
                    dve.tensor_tensor(mt[b % 2][:, :], gu_ps[:, 2 * (b % 2) + 1, :], sg[b % 2][:, :], ALU.mult)\
                       .then_inc(s["m_ready"], 1)
                    if not isinstance(n, int) or n >= 1:
                        low(h, n - 1, (b - 1) % HB)
                    if b == 3:
                        split_low(h, k + 1, nxt)

            for h in range(2):
                s = H[h]
                pair(h, 0, 0)
                pair(h, 1, 1)
                with dve.Fori(0, NPAIR // 2) as i:
                    for b in range(2):
                        k = i * 2 + (b + 2)
                        with dve.If(k <= n_pairs):
                            pair(h, k, b)
                low(h, n_pairs * HB + (HB - 1), HB - 1)
                for g in range(HB):
                    at = slice(g * BLK, (g + 1) * BLK)
                    of = slice(h * HALF + g * BLK, h * HALF + (g + 1) * BLK)
                    dve.wait_ge(s["gback_ready"], g + 1)
                    if h == 1:
                        dve.wait_ge(H[0]["res_out"], 16 * HB)
                    dve.tensor_tensor(res[:, at], gu_ps[:, g, :], s_sb[:, of], ALU.mult).then_inc(s["gs_ready"], 1)
                    dve.wait_ge(s["gs_ready"], g + 1)
                    dve.tensor_tensor(res[:, at], res[:, at], x_sb[:, of], ALU.add).then_inc(s["res_ready"], 1)

        @block.gpsimd
        def _(pool):
            pool.memset(ones[:, :], 1.0).then_inc(pool_step, 1)
            pool.wait_ge(pool_step, 1)
            pool.wait_ge(mm_ready, 1)
            pool.partition_all_reduce(mmr[:, :], mm2[:, :], P, bass.bass_isa.ReduceOp.max).then_inc(mmr_ready, 1)
            pool.wait_ge(order_ready, 3)
            n_pairs = pairs(pool.value_load(nact[0:1, 0:1], min_val=1, max_val=NE))

            def pair(h, k, b_cb):
                s = H[h]
                for b in range(HB):
                    n = k * HB + b
                    pool.wait_ge(s["m_ready"], n + 1)
                    if not isinstance(n, int) or n >= 2:
                        pool.wait_ge(s["hl_ready"], n - 1)
                    if b_cb is None:
                        pool.tensor_tensor(ht[b % 2][:, :], mt[b % 2][:, :], ones[:, :], ALU.mult)\
                            .then_inc(s["h_ready"], 1)
                    else:
                        pool.tensor_tensor(ht[b % 2][:, :], mt[b % 2][:, :], cb[b_cb][:, b * BLK:(b + 1) * BLK],
                                           ALU.mult).then_inc(s["h_ready"], 1)

            for h in range(2):
                s = H[h]
                if h == 1:
                    pool.wait_ge(H[0]["hl_ready"], (n_pairs + 1) * HB)
                pair(h, 0, None)
                pool.wait_ge(s["cb_in0"], 32)
                pair(h, 1, 0)
                with pool.Fori(0, NPAIR // 2) as i:
                    for b in range(2):
                        k = i * 2 + (b + 2)
                        with pool.If(k <= n_pairs):
                            pool.wait_ge(s[f"cb_in{1 - b}"], i * 32 + 32 * (b + 1))
                            pair(h, k, 1 - b)


def _constants():
    import numpy as np
    a = [[1, 1, 1, 0, 1, 1, 1, 0, 0, 0, 1, 1], [1, 1, 0, 1, 1, 1, 0, 0, 0, 1, 1, 0],
         [1, 0, 1, 1, 1, 0, 0, 0, 1, 1, 0, 1], [0, 1, 1, 1, 0, 0, 0, 1, 1, 0, 1, 1],
         [0, 0, 0, 0, 1, 1, 1, 1, 1, 1, 1, 1], [1, 1, 1, 1, 0, 0, 0, 0, 0, 0, 0, 0],
         [0, 0, 0, 0, 1, 1, 1, 1, 0, 0, 0, 0], [1, 1, 0, 0, 1, 1, 0, 0, 1, 1, 0, 0],
         [1, 0, 1, 0, 1, 0, 1, 0, 1, 0, 1, 0], [0, 1, 0, 1, 0, 1, 0, 1, 0, 1, 0, 1],
         [1, 0, 0, 1, 1, 0, 0, 1, 1, 0, 0, 1], [0, 1, 1, 0, 0, 1, 1, 0, 0, 1, 1, 0]]
    check = np.concatenate([np.array(a, np.float32).T, np.eye(CHECK, dtype=np.float32)], axis=1)
    c = np.zeros((P, NCONST), np.float32)
    c[:, C_IDENT:C_IDENT + P] = np.eye(P)
    k, i = np.arange(D)[:, None], np.arange(D)[None, :]
    turn = 2 * np.pi * ((k * i) % D) / D
    amp = np.where((k == 0) | (k == D // 2), np.sqrt(1 / D), np.sqrt(2 / D))
    c[:, C_DFT:C_DFT + D] = amp * np.where(k <= D // 2, np.cos(turn), np.sin(turn))
    for q in range(4):
        r = 32 * q
        c[r:r + CODE, C_HB + r:C_HB + r + CHECK] = check.T
        c[r:r + CHECK, C_WB + r:C_WB + r + CHECK] = 1
    c[:NE, C_TRI:C_TRI + NE] = np.arange(NE)[:, None] < np.arange(NE)[None, :]
    c[:, C_IOTA:C_IOTA + NE] = np.arange(NE)
    ka = np.minimum(np.arange(D), D - np.arange(D)).astype(np.float32) / np.float32(D) + np.float32(1e-8)
    c[:, C_KA] = ka
    c[:, C_KA2] = ka * ka
    c[:NE, C_EIDX] = np.arange(NE)
    c[:, C_ONE] = 1
    lx = np.log(np.array(SCALES, np.float64))
    n = len(SCALES)
    c[:, C_LX:C_LX + n] = -(n * lx - lx.sum()) / (n * (lx * lx).sum() - lx.sum() ** 2)
    return c


def kernel(L0_attn_x, L0_attn_W_el, L0_attn_b_el, L0_attn_W_le, L0_attn_b_le, L0_ffn_router_w, L0_ffn_e_bias,
           L0_ffn_Wg, L0_ffn_Wu, L0_ffn_Wd, L0_ffn_SWg, L0_ffn_SWu, L0_ffn_SWd):
    import numpy as np
    import concourse.bacc as bacc
    from concourse.bass_utils import run_bass_kernel_spmd

    x = np.ascontiguousarray(L0_attn_x)
    wle_pad = np.zeros((P, 4, D), x.dtype)
    bel_col = np.zeros((P, 1), x.dtype)
    for q in range(4):
        wle_pad[32 * q:32 * q + CODE, q] = L0_attn_W_le
        wle_pad[32 * q + CODE, q] = L0_attn_b_le
        bel_col[32 * q:32 * q + CODE, 0] = L0_attn_b_el
        bel_col[32 * q + CODE, 0] = 1
    arrays = {
        "x": x.reshape(-1, D),
        "const": _constants(),
        "w_el": np.ascontiguousarray(L0_attn_W_el),
        "wle_pad": wle_pad.reshape(P, 4 * D),
        "bel_col": bel_col,
        "router_t": np.ascontiguousarray(np.asarray(L0_ffn_router_w).T),
        "e_bias": np.asarray(L0_ffn_e_bias).reshape(1, NE),
        "wg": np.ascontiguousarray(L0_ffn_Wg),
        "wu": np.ascontiguousarray(L0_ffn_Wu),
        "wd": np.ascontiguousarray(L0_ffn_Wd),
        "shared": np.concatenate([L0_ffn_SWg, L0_ffn_SWu, L0_ffn_SWd], axis=1),
    }
    nc = bacc.Bacc("TRN2", target_bir_lowering=False, num_devices=1)
    args = {n: nc.dram_tensor(f"in_{n}", a.shape, mybir.dt.from_np(a.dtype), kind="ExternalInput").ap()
            for n, a in arrays.items()}
    out = nc.dram_tensor("out_y", arrays["x"].shape, F32, kind="ExternalOutput").ap()
    recurrent_block_kernel(nc, out=out, **args)
    r = run_bass_kernel_spmd(nc, [{f"in_{n}": a for n, a in arrays.items()}], core_ids=[0])
    return r.results[0]["out_y"].reshape(x.shape)
```

```python
from contextlib import ExitStack

import concourse.bass as bass
from concourse import mybir

ALU = mybir.AluOpType
ACT = mybir.ActivationFunctionType
AX = mybir.AxisListType
F32 = mybir.dt.float32
F32R = mybir.dt.float32r
BF16 = mybir.dt.bfloat16
I32 = mybir.dt.int32

P = 128
D = 128
CODE = 24
CHECK = 12
NE = 64
NG = 8
GE = NE // NG
TOPG = 4
DI = 64
PAIR = 2
NPAIR = NE // PAIR
SCALE = 2.5
LN_EPS = 1e-5
FD_EPS = 1e-10
SCALES = (2, 4, 8, 16, 32)
BIG = 3.0e38
SIG_HALF = 2.0 ** -24

C_IDENT = 0
C_DFT = 128
C_HB = 256
C_WB = 384
C_TRI = 512
C_IOTA = 576
C_KA = 640
C_KA2 = 641
C_EIDX = 642
C_ONE = 643
C_LX = 644
NCONST = 652


def recurrent_block_kernel(nc, x, const, w_el, wle_pad, bel_col, router_t, e_bias, wgu, wd, shared, out):
    T = x.shape[0]
    NT = T // P
    NCH = 4
    CT = NT // NCH
    QT = NT // 4
    BLK = 512
    TB = BLK // P
    NB = T // BLK
    HALF = T // 2
    HB = HALF // BLK
    ND = 2 * HB

    x_rows = x.rearrange("(p j) e -> p (j e)", j=NT)
    out_rows = out.rearrange("(p j) e -> p (j e)", j=NT)
    coef_dram = nc.dram_tensor("coef_by_expert", [NE, T], F32).ap()

    with ExitStack() as ctx:
        def sb(name, shape, dt=F32):
            return ctx.enter_context(nc.sbuf_tensor(name, shape, dt))

        def sem(name):
            return ctx.enter_context(nc.semaphore(name))

        gu_ps = ctx.enter_context(nc.psum_tensor("gu_ps", [P, 4, BLK], F32))
        y_ps = ctx.enter_context(nc.psum_tensor("y_ps", [P, 4, BLK], F32))

        x_sb = sb("x_sb", [P, NT * D])
        cst = sb("cst", [P, NCONST])
        wel_sb = sb("wel_sb", [P, CODE])
        wle_sb = sb("wle_sb", [P, 4 * D])
        bel_sb = sb("bel_sb", [P, 1])
        rt_sb = sb("rt_sb", [P, NE])
        eb_sb = sb("eb_sb", [P, NE])
        bn6 = sb("bn6", [P, NT, 6])
        mv = sb("mv", [P, NT, 2])
        std = sb("std", [P, NT])
        rstd = sb("rstd", [P, NT])
        xn = sb("xn", [P, NT * D])
        xh = sb("xh", [P, T], F32R)
        xl = sb("xl", [P, T], F32R)
        mm = sb("mm", [P, 2, NCH])
        mm2 = sb("mm2", [P, 2])
        mmr = sb("mmr", [P, 2])
        den = sb("den", [1, 2])
        blk = sb("blk", [1, 1024])
        over = sb("over", [1, 1024])
        sums = sb("sums", [1, 8])
        cnt = sb("cnt", [1, 8])
        dim = sb("dim", [1, 4])
        dimc = sb("dimc", [P, 1])
        ang = sb("ang", [P, 12])
        dft_f = sb("dft_f", [P, D])
        circ = sb("circ", [P, D])
        circ_h = sb("circ_h", [P, D], F32R)
        circ_l = sb("circ_l", [P, D], F32R)
        cel_h = sb("cel_h", [P, 4, D], F32R)
        cel_l = sb("cel_l", [P, 4, D], F32R)
        hb_bf = sb("hb_bf", [P, P], BF16)
        wb_bf = sb("wb_bf", [P, P], BF16)
        bits = sb("bits", [P, 2 * BLK], BF16)
        syn = sb("syn", [P, 2 * BLK], BF16)
        pat = sb("pat", [P, 2 * BLK], BF16)
        corr = sb("corr", [P, 2 * BLK], F32R)
        wle_h = sb("wle_h", [P, 4 * D], F32R)
        wle_l = sb("wle_l", [P, 4 * D], F32R)
        s_sb = sb("s_sb", [P, NT * D])
        rt_h = sb("rt_h", [P, NE], F32R)
        rt_l = sb("rt_l", [P, NE], F32R)
        score = sb("score", [P, NT, NE])
        sfc = sb("sfc", [P, CT, NE])
        hi4 = sb("hi4", [P, CT * NG, 4])
        lo4 = sb("lo4", [P, CT * NG, 4])
        hi2 = sb("hi2", [P, CT * NG, 2])
        lo2 = sb("lo2", [P, CT * NG, 2])
        lo2b = sb("lo2b", [P, CT * NG, 2])
        top1 = sb("top1", [P, CT * NG])
        sec1 = sb("sec1", [P, CT * NG])
        sec2 = sb("sec2", [P, CT * NG])
        gsx = sb("gsx", [P, CT, TOPG + NG])
        gtop = sb("gtop", [P, CT, 8])
        gtaken = sb("gtaken", [P, CT, TOPG + NG])
        gmask = sb("gmask", [P, CT * NG])
        masked = sb("masked", [P, CT, NE])
        etop = sb("etop", [P, CT, 8])
        taken = sb("taken", [P, CT, NE])
        anyc = sb("anyc", [P, NCH, NE])
        used = sb("used", [P, NCH, NE])
        wsel = sb("wsel", [P, CT, NE])
        wsum = sb("wsum", [P, CT])
        winv = sb("winv", [P, CT])
        coef = sb("coef", [P, 2, CT, NE])
        coef_t = sb("coef_t", [P, NCH, BLK])
        act_c = sb("act_c", [NE, 1])
        rk = sb("rk", [NE, 6])
        place = sb("place", [NE, NE])
        order = sb("order", [1, NE + 2 * PAIR], I32)
        nact = sb("nact", [1, 1], I32)
        WP = 3 * D
        raw = sb("raw", [P, WP])
        sraw = sb("sraw", [P, WP])
        sw_h = sb("sw_h", [P, WP], F32R)
        sw_l = sb("sw_l", [P, WP], F32R)
        w_h = [sb(f"w_h{b}", [P, WP], F32R) for b in range(2)]
        w_l = [sb(f"w_l{b}", [P, WP], F32R) for b in range(2)]
        cb = [sb(f"cb{b}", [P, HALF]) for b in range(2)]
        ones = sb("ones", [P, BLK])
        sg = [sb(f"sg{b}", [P, BLK]) for b in range(2)]
        mt = [sb(f"mt{b}", [P, BLK]) for b in range(2)]
        ht = [sb(f"ht{b}", [P, BLK]) for b in range(2)]
        hh = [sb(f"hh{b}", [P, BLK], F32R) for b in range(2)]
        hl = [sb(f"hl{b}", [P, BLK], F32R) for b in range(2)]
        res = xn[:, 0:HALF]
        gt = xn[:, HALF:T].rearrange("p (b n) -> p b n", n=BLK)

        ident = cst[:, C_IDENT:C_IDENT + P]
        dft = cst[:, C_DFT:C_DFT + D]

        x_in = [sem(f"x_in{c}") for c in range(NCH)]
        cst_in = sem("cst_in")
        small_in = sem("small_in")
        dve_step = sem("dve_step")
        act_step = sem("act_step")
        pool_step = sem("pool_step")
        var_ready = sem("var_ready")
        std_ready = sem("std_ready")
        xn_ready = sem("xn_ready")
        xt_ready = sem("xt_ready")
        xh_ready = sem("xh_ready")
        xl_ready = sem("xl_ready")
        rt_h_ready = sem("rt_h_ready")
        rt_l_ready = sem("rt_l_ready")
        logit_ready = sem("logit_ready")
        score_ready = sem("score_ready")
        mm_ready = sem("mm_ready")
        mmr_ready = sem("mmr_ready")
        cnt_ready = sem("cnt_ready")
        ln_ready = sem("ln_ready")
        dim_ready = sem("dim_ready")
        dimb_ready = sem("dimb_ready")
        ang_ready = sem("ang_ready")
        sin_ready = sem("sin_ready")
        dftf_ready = sem("dftf_ready")
        circ_ps_ready = sem("circ_ps_ready")
        circ_ready = sem("circ_ready")
        circ_h_ready = sem("circ_h_ready")
        circ_l_ready = sem("circ_l_ready")
        cel_ps_ready = sem("cel_ps_ready")
        cel_h_ready = sem("cel_h_ready")
        cel_l_ready = sem("cel_l_ready")
        zero_ready = sem("zero_ready")
        hbwb_ready = sem("hbwb_ready")
        wle_h_ready = sem("wle_h_ready")
        wle_l_ready = sem("wle_l_ready")
        lat_ready = sem("lat_ready")
        bits_ready = sem("bits_ready")
        syn_ps_ready = sem("syn_ps_ready")
        syn_ready = sem("syn_ready")
        wt_ps_ready = sem("wt_ps_ready")
        corr_ready = sem("corr_ready")
        s_ps_ready = sem("s_ps_ready")
        s_ready = sem("s_ready")
        coef_ready = sem("coef_ready")
        coeft_ps_ready = sem("coeft_ps_ready")
        coeft_ready = sem("coeft_ready")
        coeft_out = [sem(f"coeft_out{c}") for c in range(NCH)]
        used_ready = sem("used_ready")
        used_ps_ready = sem("used_ps_ready")
        active_ready = sem("active_ready")
        rank_ps_ready = sem("rank_ps_ready")
        place_ready = sem("place_ready")
        order_ps_ready = sem("order_ps_ready")
        order_ready = sem("order_ready")
        sw_h_ready = sem("sw_h_ready")
        sw_l_ready = sem("sw_l_ready")
        H = []
        for h in range(2):
            H.append({n: sem(f"{n}_{h}") for n in (
                "raw_in", "cb_in0", "cb_in1", "w_h_ready", "w_l_ready", "g_ready", "u_ready", "silu_ready",
                "m_ready", "h_ready", "hh_ready", "hl_ready", "down_done", "gt_ready", "gback_ready",
                "gs_ready", "res_ready", "res_out")})

        block = ctx.enter_context(nc.Block())
        listing = y_ps[:, 3, :]

        def tile(buf, j):
            return buf[:, j * D:(j + 1) * D]

        def blocks_of(h, b):
            return slice(h * HALF + b * BLK, h * HALF + (b + 1) * BLK)

        def pairs(n_active):
            return (n_active + 1) // 2

        UN = 4

        def later_pairs(eng, n_pairs, body):
            def step(i, u):
                k = i * UN + (u + 2)
                with eng.If(k <= n_pairs):
                    body(k, i, u)
                    if u + 1 < UN:
                        step(i, u + 1)

            with eng.Fori(0, NPAIR // UN) as i:
                step(i, 0)

        @block.sync
        def _(sp):
            sp.dma_start(cst[:, :], const).then_inc(cst_in, 16)
            w = CT * D
            for c in range(NCH):
                sp.dma_start(x_sb[:, c * w:(c + 1) * w], x_rows[:, c * w:(c + 1) * w]).then_inc(x_in[c], 16)
            for dst, src in ((rt_sb, router_t), (wel_sb, w_el), (wle_sb, wle_pad), (bel_sb, bel_col), (sraw, shared)):
                sp.dma_start(dst[:, :], src).then_inc(small_in, 16)
            sp.dma_start(eb_sb[:, :], e_bias.to_broadcast([P, NE])).then_inc(small_in, 16)
            by_tile = coef_dram.rearrange("e (c t a p) -> e c t a p", c=NCH, a=2, p=P)
            for c in range(NCH):
                sp.wait_ge(coeft_ready, c + 1)
                for a in range(2):
                    sp.dma_start(by_tile[:, c, :, a, :],
                                 coef_t[a * NE:(a + 1) * NE, c, :].rearrange("e (t p) -> e t p", p=P)
                                 ).then_inc(coeft_out[c], 16)
            for c in range(NCH):
                sp.wait_ge(coeft_out[c], 32)
            sp.wait_ge(order_ready, 2)
            n_pairs = pairs(sp.value_load(nact[0:1, 0:1], min_val=1, max_val=NE))

            def experts(k):
                return [sp.value_load(order[0:1, bass.ds(PAIR * (k - 1) + m, 1)], min_val=0, max_val=NE - 1)
                        for m in range(PAIR)]

            gate_up = raw[:, 0:2 * D].rearrange("p (what m i) -> p m what i", what=2, m=PAIR)

            def load_weights(h, chosen):
                s = H[h]
                for m, e in enumerate(chosen):
                    pick = bass.ds(e, 1)
                    sp.dma_start(gate_up[:, m], wgu[pick].rearrange("a h w i -> (a h) w i")).then_inc(s["raw_in"], 16)
                    sp.dma_start(raw[m * DI:(m + 1) * DI, 2 * D:3 * D],
                                 wd[pick].rearrange("a i h -> (a i) h")).then_inc(s["raw_in"], 16)

            def load_coefs(h, chosen, b):
                for m, e in enumerate(chosen):
                    sp.dma_start(cb[b][m * DI:(m + 1) * DI, :],
                                 coef_dram[bass.ds(e, 1), h * HALF:(h + 1) * HALF].to_broadcast([DI, HALF])
                                 ).then_inc(H[h][f"cb_in{b}"], 16)

            def store_results(h):
                for g in range(HB):
                    sp.wait_ge(H[h]["res_ready"], g + 1)
                    at = slice(h * HALF + g * BLK, h * HALF + (g + 1) * BLK)
                    sp.dma_start(out_rows[:, at], res[:, g * BLK:(g + 1) * BLK]).then_inc(H[h]["res_out"], 16)

            for h in range(2):
                s = H[h]
                chosen = experts(1)
                if h == 1:
                    o = H[0]
                    sp.wait_ge(o["w_l_ready"], n_pairs + 1)
                load_weights(h, chosen)
                if h == 1:
                    sp.wait_ge(o["h_ready"], (n_pairs + 1) * HB)
                    sp.wait_ge(o["cb_in0"], (n_pairs + 2) // 2 * 32)
                    sp.wait_ge(o["cb_in1"], (n_pairs + 1) // 2 * 32)
                load_coefs(h, chosen, 0)

                def load_next(k, b):
                    chosen = experts(k + 1)
                    sp.wait_ge(s["w_l_ready"], k)
                    load_weights(h, chosen)
                    sp.wait_ge(s["h_ready"], k * HB)
                    load_coefs(h, chosen, b)

                load_next(1, 1)
                if h == 1:
                    store_results(0)
                later_pairs(sp, n_pairs, lambda k, i, u: load_next(k, u % 2))
            store_results(1)
            for h in range(2):
                sp.wait_ge(H[h]["res_out"], 16 * HB)

        @block.tensor
        def _(pe):
            def mm3(out_ap, lhs, rhs, start=True):
                (lh, ll), (rh, rl) = lhs, rhs
                pe.matmul(out_ap, ll, rh, start=start, stop=False, skip_group_check=True)
                pe.matmul(out_ap, lh, rl, start=False, stop=False, skip_group_check=True)
                return pe.matmul(out_ap, lh, rh, start=False, stop=True, skip_group_check=True)

            pe.wait_ge(cst_in, 16)

            def transposes(g):
                pe.wait_ge(xn_ready, g // 2 + 1)
                if g >= 4:
                    pe.wait_ge(xl_ready, g - 3)
                for t in range(TB):
                    last = pe.transpose(gu_ps[:, g % 4, t * P:(t + 1) * P], tile(xn, g * TB + t), ident)
                last.then_inc(xt_ready, 1)

            def logits(g):
                pe.wait_ge(xl_ready, g + 1)
                if g == 0:
                    pe.wait_ge(rt_l_ready, 1)
                for t in range(TB):
                    j = g * TB + t
                    at = j % CT * NE
                    last = mm3(y_ps[:, j // CT, at:at + NE], (tile(xh, j), tile(xl, j)), (rt_h[:, :], rt_l[:, :]))
                last.then_inc(logit_ready, 1)

            for g in range(NB + 1):
                if g < NB:
                    transposes(g)
                if g >= 1:
                    logits(g - 1)

            misc = gu_ps[:, 3, :]
            pe.wait_ge(xl_ready, NB)
            pe.wait_ge(dim_ready, 1)
            pe.matmul(misc[:, 0:1], cst[0:1, C_ONE:C_ONE + 1].to_broadcast([1, P]), dim[0:1, 3:4], start=True, stop=True).then_inc(dimb_ready, 1)
            pe.wait_ge(dftf_ready, 1)
            pe.matmul(misc[:, 128:256], dft_f[:, :], dft, start=True, stop=True).then_inc(circ_ps_ready, 1)
            pe.wait_ge(circ_ready, 1)
            pe.matmul(misc[:, 256:256 + CODE], circ[:, :], wel_sb[:, :], start=True, stop=True).then_inc(cel_ps_ready, 1)
            pe.wait_ge(cel_l_ready, 1)
            for c in range(2):
                for q in range(4):
                    at = slice(q * QT * P + c * BLK, q * QT * P + (c + 1) * BLK)
                    o = gu_ps[:, c, :]
                    pe.matmul(o, cel_l[:, q, :], xh[:, at], start=(q == 0), stop=False)
                    pe.matmul(o, cel_h[:, q, :], xl[:, at], start=False, stop=False)
                    last = pe.matmul(o, cel_h[:, q, :], xh[:, at], start=False, stop=(q == 3))
                last.then_inc(lat_ready, 1)
            pe.wait_ge(hbwb_ready, 2)
            for c in range(2):
                pe.wait_ge(bits_ready, c + 1)
                pe.matmul(gu_ps[:, 2 + c, :], hb_bf[:, :], bits[:, c * BLK:(c + 1) * BLK],
                          start=True, stop=True).then_inc(syn_ps_ready, 1)
            for c in range(2):
                pe.wait_ge(syn_ready, c + 1)
                pe.matmul(gu_ps[:, c, :], wb_bf[:, :], syn[:, c * BLK:(c + 1) * BLK],
                          start=True, stop=True).then_inc(wt_ps_ready, 1)
            pe.wait_ge(circ_l_ready, 1)
            pe.wait_ge(wle_l_ready, 1)
            pe.wait_ge(corr_ready, 2)
            for g in range(NB):
                if g >= 4:
                    pe.wait_ge(s_ready, g - 3)
                for t in range(TB):
                    j = g * TB + t
                    q, c = divmod(j, QT)
                    o = gu_ps[:, g % 4, t * D:(t + 1) * D]
                    mm3(o, (tile(xh, j), tile(xl, j)), (circ_h[:, :], circ_l[:, :]))
                    cc = corr[:, c * P:(c + 1) * P]
                    pe.matmul(o, cc, wle_l[:, q * D:(q + 1) * D], start=False, stop=False, skip_group_check=True)
                    last = pe.matmul(o, cc, wle_h[:, q * D:(q + 1) * D], start=False, stop=True,
                                     skip_group_check=True)
                last.then_inc(s_ps_ready, 1)
            for c in range(NCH):
                pe.wait_ge(coef_ready, c + 1)
                pe.wait_ge(score_ready, c + 1)
                for t in range(CT // 2):
                    last = pe.transpose(y_ps[:, c, t * P:(t + 1) * P],
                                        coef[:, c % 2, 2 * t:2 * t + 2, :].rearrange("p t e -> p (t e)"), ident)
                last.then_inc(coeft_ps_ready, 1)
            S = (sw_h, sw_l)
            W = [(w_h[b], w_l[b]) for b in range(2)]

            def count_uses():
                pe.wait_ge(coeft_ready, NCH)
                pe.wait_ge(used_ready, 1)
                for c in range(NCH):
                    last = pe.matmul(listing[0:NE, 0:1], used[:, c, :], cst[:, C_ONE:C_ONE + 1], start=(c == 0),
                                     stop=(c == NCH - 1))
                last.then_inc(used_ps_ready, 1)

            def rank():
                pe.wait_ge(active_ready, 1)
                pe.matmul(listing[0:NE, 8:9], cst[0:NE, C_TRI:C_TRI + NE], act_c[:, :], start=True, stop=True)
                pe.matmul(listing[0:NE, 9:10], cst[0:NE, C_ONE:C_ONE + 1].to_broadcast([NE, NE]), act_c[:, :],
                          start=True, stop=True).then_inc(rank_ps_ready, 1)

            def list_experts():
                pe.wait_ge(place_ready, 1)
                pe.matmul(listing[0:1, 64:64 + NE], cst[0:NE, C_EIDX:C_EIDX + 1], place[:, :],
                          start=True, stop=True).then_inc(order_ps_ready, 1)

            def down(h, n, b, w, first):
                s = H[h]
                pe.wait_ge(s["hl_ready"], n + 1)
                if first and h == 1:
                    pe.wait_ge(H[0]["gs_ready"], b + 1)
                wh, wl = (v[:, 2 * D:3 * D] for v in w)
                mm3(y_ps[:, b, :], (wh, wl), (hh[b % 2][:, :], hl[b % 2][:, :]),
                    start=first).then_inc(s["down_done"], 1)

            def gate_up(h, n, b, w):
                s = H[h]
                if not isinstance(n, int) or n >= 2:
                    pe.wait_ge(s["m_ready"], n - 1)
                at = blocks_of(h, b)
                for what, name in ((0, "g_ready"), (1, "u_ready")):
                    wh, wl = (v[:, what * D:(what + 1) * D] for v in w)
                    mm3(gu_ps[:, 2 * (b % 2) + what, :], (wh, wl), (xh[:, at], xl[:, at])).then_inc(s[name], 1)

            def pair(h, k, w, before):
                for b in range(HB):
                    n = k * HB + b
                    gate_up(h, n, b, w)
                    if b >= 2:
                        down(h, n - 2, b - 2, w, False)
                    else:
                        down(h, n - 2, b + 2, before, before is S)

            def down_last(h, b):
                n = n_pairs * HB + b
                with pe.If((n_pairs % 2) > 0):
                    down(h, n, b, W[0], False)
                with pe.Else():
                    down(h, n, b, W[1], False)

            def turn_back(h, g):
                pe.wait_ge(H[h]["gt_ready"], g + 1)
                for t in range(TB):
                    last = pe.transpose(y_ps[:, g, t * P:(t + 1) * P], gt[:, g, t * P:(t + 1) * P], ident)
                last.then_inc(H[h]["gback_ready"], 1)

            def rest_of_half(h):
                s = H[h]
                pe.wait_ge(s["w_l_ready"], 1)
                pair(h, 1, W[0], S)

                def one(k, i, u):
                    pe.wait_ge(s["w_l_ready"], k)
                    pair(h, k, W[1 - u % 2], W[u % 2])

                later_pairs(pe, n_pairs, one)

            pe.wait_ge(sw_l_ready, 1)
            pe.wait_ge(s_ready, NB)
            count_uses()
            gate_up(0, 0, 0, S)
            rank()
            gate_up(0, 1, 1, S)
            list_experts()
            gate_up(0, 2, 2, S)
            down(0, 0, 0, S, True)
            gate_up(0, 3, 3, S)
            pe.wait_ge(order_ready, 2)
            down(0, 1, 1, S, True)
            n_pairs = pairs(pe.value_load(nact[0:1, 0:1], min_val=1, max_val=NE))
            rest_of_half(0)
            last_n = n_pairs * HB
            pe.wait_ge(H[0]["m_ready"], last_n + 3)
            gate_up(1, 0, 0, S)
            down_last(0, 2)
            pe.wait_ge(H[0]["m_ready"], last_n + 4)
            gate_up(1, 1, 1, S)
            down_last(0, 3)
            turn_back(0, 0)
            turn_back(0, 1)
            gate_up(1, 2, 2, S)
            turn_back(0, 2)
            down(1, 0, 0, S, True)
            gate_up(1, 3, 3, S)
            turn_back(0, 3)
            down(1, 1, 1, S, True)
            rest_of_half(1)
            down_last(1, 2)
            turn_back(1, 0)
            down_last(1, 3)
            for g in range(1, HB):
                turn_back(1, g)

        @block.scalar
        def _(act):
            def chain(ins, count):
                ins.then_inc(act_step, 1)
                act.wait_ge(act_step, count)

            act.wait_ge(small_in, 96)
            act.activation(rt_h[:, :], rt_sb[:, :], ACT.Copy).then_inc(rt_h_ready, 1)
            act.activation(sw_h[:, :], sraw[:, :], ACT.Copy).then_inc(sw_h_ready, 1)
            act.activation(wle_h[:, :], wle_sb[:, :], ACT.Copy).then_inc(wle_h_ready, 1)
            for c in range(NCH):
                act.wait_ge(var_ready, c + 1)
                act.activation(std[:, c * CT:(c + 1) * CT], mv[:, c * CT:(c + 1) * CT, 1], ACT.Sqrt,
                               ).then_inc(std_ready, 1)
            for g in range(NB):
                act.wait_ge(xt_ready, g + 1)
                act.activation(xh[:, g * BLK:(g + 1) * BLK], gu_ps[:, g % 4, :], ACT.Copy).then_inc(xh_ready, 1)
            for c in range(NCH):
                act.wait_ge(logit_ready, 2 * c + 2)
                act.activation(score[:, c * CT:(c + 1) * CT, :].rearrange("p t e -> p (t e)"), y_ps[:, c, :],
                               ACT.Sigmoid).then_inc(score_ready, 1)
            act.wait_ge(cnt_ready, 1)
            act.activation(cnt[0:1, 0:5], sums[0:1, 0:5], ACT.Ln).then_inc(ln_ready, 1)
            act.wait_ge(ang_ready, 1)
            act.activation(ang[:, 6:8], ang[:, 4:6], ACT.Sin).then_inc(sin_ready, 1)
            act.wait_ge(circ_ps_ready, 1)
            act.activation(circ[:, :], gu_ps[:, 3, 128:256], ACT.Copy).then_inc(circ_ready, 1)
            act.wait_ge(circ_ready, 1)
            act.activation(circ_h[:, :], circ[:, :], ACT.Copy).then_inc(circ_h_ready, 1)
            act.wait_ge(cel_ps_ready, 1)
            act.wait_ge(zero_ready, 1)
            for q in range(4):
                last = act.activation(cel_h[:, q, 32 * q:32 * q + CODE], gu_ps[:, 3, 256:256 + CODE], ACT.Copy)
            last.then_inc(cel_h_ready, 1)
            for g in range(NB):
                act.wait_ge(s_ps_ready, g + 1)
                act.activation(s_sb[:, g * BLK:(g + 1) * BLK], gu_ps[:, g % 4, :], ACT.Copy).then_inc(s_ready, 1)
            for c in range(NCH):
                act.wait_ge(coeft_ps_ready, c + 1)
                act.activation(coef_t[:, c, :], y_ps[:, c, :], ACT.Copy).then_inc(coeft_ready, 1)

            def split_high(h, k, b):
                s = H[h]
                act.wait_ge(s["raw_in"], 64 * k)
                act.activation(w_h[b][:, :], raw[:, :], ACT.Copy).then_inc(s["w_h_ready"], 1)

            def high(h, n, b):
                s = H[h]
                if isinstance(n, int) and n < 2:
                    if h == 1:
                        act.wait_ge(H[0]["down_done"], last_n + (n + 3))
                else:
                    act.wait_ge(s["down_done"], n - 1)
                act.wait_ge(s["h_ready"], n + 1)
                act.activation(hh[b % 2][:, :], ht[b % 2][:, :], ACT.Copy).then_inc(s["hh_ready"], 1)

            def silu(h, n, b):
                s = H[h]
                act.wait_ge(s["g_ready"], n + 1)
                act.activation(sg[b % 2][:, :], gu_ps[:, 2 * (b % 2), :], ACT.Silu).then_inc(s["silu_ready"], 1)

            def pair(h, k, nxt):
                for b in range(HB):
                    n = k * HB + b
                    silu(h, n, b)
                    high(h, n - 1, (b - 1) % HB)
                    if b == 2:
                        if not isinstance(k, int) or k >= 2:
                            act.wait_ge(H[h]["down_done"], k * HB)
                        split_high(h, k + 1, nxt)

            def activate(h, g):
                act.wait_ge(H[h]["down_done"], last_n + (g + 1))
                act.activation(gt[:, g, :], y_ps[:, g, :], ACT.Silu).then_inc(H[h]["gt_ready"], 1)

            def rest_of_half(h):
                pair(h, 1, 1)
                later_pairs(act, n_pairs, lambda k, i, u: pair(h, k, u % 2))

            silu(0, 0, 0)
            silu(0, 1, 1)
            high(0, 0, 0)
            silu(0, 2, 2)
            high(0, 1, 1)
            silu(0, 3, 3)
            high(0, 2, 2)
            split_high(0, 1, 0)
            act.wait_ge(order_ready, 2)
            n_pairs = pairs(act.value_load(nact[0:1, 0:1], min_val=1, max_val=NE))
            last_n = n_pairs * HB
            rest_of_half(0)
            silu(1, 0, 0)
            high(0, last_n + 3, 3)
            activate(0, 0)
            activate(0, 1)
            silu(1, 1, 1)
            high(1, 0, 0)
            activate(0, 2)
            activate(0, 3)
            silu(1, 2, 2)
            high(1, 1, 1)
            split_high(1, 1, 0)
            silu(1, 3, 3)
            high(1, 2, 2)
            rest_of_half(1)
            activate(1, 0)
            high(1, last_n + 3, 3)
            for g in range(1, HB):
                activate(1, g)

        @block.vector
        def _(dve):
            steps = [0]

            def then(ins):
                steps[0] += 1
                ins.then_inc(dve_step, 1)
                dve.wait_ge(dve_step, steps[0])

            dve.memset(cel_h[:, :, :].rearrange("p q c -> p (q c)").bitcast(F32), 0.0)
            dve.memset(order[:, :], 0)
            then(dve.memset(cel_l[:, :, :].rearrange("p q c -> p (q c)").bitcast(F32), 0.0))
            dve.memset(gsx[:, :, :], BIG).then_inc(zero_ready, 1)
            dve.wait_ge(cst_in, 16)
            for c in range(NCH):
                dve.wait_ge(x_in[c], 16)
                tiles = range(c * CT, (c + 1) * CT)
                cs = slice(c * CT, (c + 1) * CT)
                for j in tiles:
                    last = dve.bn_stats(bn6[:, j, :], tile(x_sb, j))
                then(last)
                for j in tiles:
                    last = dve.bn_aggr(mv[:, j, :], bn6[:, j, :])
                then(last)
                then(dve.tensor_scalar(mv[:, cs, 1], mv[:, cs, 1], LN_EPS, None, ALU.add))
                dve.tensor_copy(rstd[:, cs], mv[:, cs, 1]).then_inc(var_ready, 1)
                dve.wait_ge(std_ready, c + 1)
                then(dve.reciprocal(rstd[:, cs], std[:, cs]))
                then(dve.tensor_tensor(std[:, cs], rstd[:, cs], rstd[:, cs], ALU.mult))
                then(dve.tensor_tensor(std[:, cs], std[:, cs], mv[:, cs, 1], ALU.mult))
                then(dve.tensor_scalar(std[:, cs], std[:, cs], -0.5, 1.5, ALU.mult, ALU.add))
                then(dve.tensor_tensor(rstd[:, cs], rstd[:, cs], std[:, cs], ALU.mult))
                for j in tiles:
                    last = dve.tensor_scalar(tile(xn, j), tile(x_sb, j), mv[:, j, 0:1], rstd[:, j:j + 1],
                                             ALU.subtract, ALU.mult)
                last.then_inc(xn_ready, 1)
                if c == 0:
                    dve.wait_ge(rt_h_ready, 1)
                    dve.tensor_tensor(rt_l[:, :], rt_sb[:, :], rt_h[:, :].bitcast(F32), ALU.subtract)\
                       .then_inc(rt_l_ready, 1)
                dve.wait_ge(xn_ready, c + 1)
                w = slice(c * CT * D, (c + 1) * CT * D)
                dve.tensor_reduce(mm[:, 0, c:c + 1], xn[:, w], AX.X, ALU.max)
                last = dve.tensor_reduce(mm[:, 1, c:c + 1], xn[:, w], AX.X, ALU.min)
            then(last)
            then(dve.tensor_reduce(mm2[:, 0:1], mm[:, 0, :], AX.X, ALU.max))
            then(dve.tensor_reduce(mm2[:, 1:2], mm[:, 1, :], AX.X, ALU.min))
            dve.tensor_scalar(mm2[:, 1:2], mm2[:, 1:2], -1.0, None, ALU.mult).then_inc(mm_ready, 1)
            for g in range(NB):
                dve.wait_ge(xh_ready, g + 1)
                at = slice(g * BLK, (g + 1) * BLK)
                dve.tensor_tensor(xl[:, at], gu_ps[:, g % 4, :], xh[:, at].bitcast(F32), ALU.subtract)\
                   .then_inc(xl_ready, 1)
            dve.wait_ge(mmr_ready, 1)
            then(dve.tensor_scalar(den[0:1, 0:1], mmr[0:1, 0:1], mmr[0:1, 1:2], FD_EPS, ALU.add, ALU.add))
            then(dve.reciprocal(den[0:1, 1:2], den[0:1, 0:1]))
            then(dve.tensor_scalar(blk[:, :], xn[0:1, 0:1024], mmr[0:1, 1:2], den[0:1, 1:2], ALU.add, ALU.mult))
            for i, sc in enumerate(SCALES):
                last = dve.tensor_reduce(sums[0:1, i:i + 1], blk[0:1, 0:sc * sc], AX.X, ALU.add)
            then(last)
            for i, sc in enumerate(SCALES):
                last = dve.tensor_scalar(cnt[0:1, i:i + 1], sums[0:1, i:i + 1], 1.0 / (sc * sc), None, ALU.mult)
            then(last)
            for i, sc in enumerate(SCALES):
                then(dve.tensor_scalar(over[0:1, 0:sc * sc], blk[0:1, 0:sc * sc], cnt[0:1, i:i + 1], None, ALU.is_gt))
                then(dve.tensor_reduce(sums[0:1, i:i + 1], over[0:1, 0:sc * sc], AX.X, ALU.add))
            dve.tensor_scalar(sums[0:1, 0:5], sums[0:1, 0:5], 1.0, None, ALU.max).then_inc(cnt_ready, 1)
            dve.wait_ge(ln_ready, 1)
            then(dve.tensor_tensor(sums[0:1, 0:5], cnt[0:1, 0:5], cst[0:1, C_LX:C_LX + 5], ALU.mult))
            then(dve.tensor_reduce(dim[0:1, 0:1], sums[0:1, 0:5], AX.X, ALU.add))
            dve.tensor_scalar(dim[0:1, 3:4], dim[0:1, 0:1], 1.0, 2.0, ALU.max, ALU.min).then_inc(dim_ready, 1)
            dve.wait_ge(dimb_ready, 1)
            then(dve.tensor_copy(dimc[:, :], gu_ps[:, 3, 0:1]))
            dcol, ka, ka2 = dimc[:, 0:1], cst[:, C_KA:C_KA + 1], cst[:, C_KA2:C_KA2 + 1]
            dve.tensor_scalar(ang[:, 0:1], dcol, 0.2, 1.0, ALU.mult, ALU.add)
            dve.tensor_scalar(ang[:, 1:2], dcol, 0.5, 1.0, ALU.mult, ALU.add)
            then(dve.tensor_scalar(ang[:, 2:3], dcol, 0.1, None, ALU.mult))
            dve.tensor_tensor(ang[:, 0:1], ang[:, 0:1], dcol, ALU.mult)
            dve.tensor_tensor(ang[:, 1:2], ang[:, 1:2], ka, ALU.mult)
            then(dve.tensor_tensor(ang[:, 3:4], ang[:, 2:3], ka2, ALU.mult))
            dve.tensor_tensor(ang[:, 8:9], ang[:, 0:1], ang[:, 1:2], ALU.add)
            then(dve.tensor_tensor(ang[:, 9:10], ang[:, 0:1], ka, ALU.subtract))
            then(dve.tensor_tensor(ang[:, 10:11], ang[:, 9:10], ang[:, 3:4], ALU.add))
            dve.tensor_scalar(ang[:, 4:5], ang[:, 8:9], -1.0, 3.14159265358979, ALU.mult, ALU.add)
            dve.tensor_scalar(ang[:, 5:6], ang[:, 10:11], -1.0, 1.5707963267949, ALU.mult, ALU.add)\
               .then_inc(ang_ready, 1)
            dve.wait_ge(sin_ready, 1)
            dve.tensor_scalar(dft_f[:, :], dft, ang[:, 6:7], ang[:, 7:8], ALU.mult, ALU.mult).then_inc(dftf_ready, 1)
            dve.wait_ge(small_in, 96)
            dve.tensor_copy(hb_bf[:, :], cst[:, C_HB:C_HB + P]).then_inc(hbwb_ready, 1)
            dve.tensor_copy(wb_bf[:, :], cst[:, C_WB:C_WB + P]).then_inc(hbwb_ready, 1)
            dve.wait_ge(wle_h_ready, 1)
            dve.tensor_tensor(wle_l[:, :], wle_sb[:, :], wle_h[:, :].bitcast(F32), ALU.subtract).then_inc(wle_l_ready, 1)
            dve.wait_ge(sw_h_ready, 1)
            dve.tensor_tensor(sw_l[:, :], sraw[:, :], sw_h[:, :].bitcast(F32), ALU.subtract).then_inc(sw_l_ready, 1)
            dve.wait_ge(circ_h_ready, 1)
            dve.tensor_tensor(circ_l[:, :], circ[:, :], circ_h[:, :].bitcast(F32), ALU.subtract).then_inc(circ_l_ready, 1)
            dve.wait_ge(cel_h_ready, 1)
            for q in range(4):
                at = slice(32 * q, 32 * q + CODE)
                last = dve.tensor_tensor(cel_l[:, q, at], gu_ps[:, 3, 256:256 + CODE], cel_h[:, q, at].bitcast(F32),
                                         ALU.subtract)
            last.then_inc(cel_l_ready, 1)
            for c in range(2):
                dve.wait_ge(lat_ready, c + 1)
                dve.tensor_scalar(bits[:, c * BLK:(c + 1) * BLK], gu_ps[:, c, :], bel_sb[:, 0:1], SIG_HALF,
                                  ALU.add, ALU.is_gt).then_inc(bits_ready, 1)
            for c in range(2):
                dve.wait_ge(syn_ps_ready, c + 1)
                dve.tensor_scalar(syn[:, c * BLK:(c + 1) * BLK], gu_ps[:, 2 + c, :], 0.5, None, ALU.is_gt)\
                   .then_inc(syn_ready, 1)
            for c in range(2):
                at = slice(c * BLK, (c + 1) * BLK)
                dve.wait_ge(wt_ps_ready, c + 1)
                then(dve.scalar_tensor_tensor(pat[:, at], gu_ps[:, c, :], 3.5, syn[:, at], ALU.is_le, ALU.mult))
                dve.tensor_tensor(corr[:, at], bits[:, at], pat[:, at], ALU.not_equal).then_inc(corr_ready, 1)

            for c in range(NCH):
                sc = score[:, c * CT:(c + 1) * CT, :]
                dve.wait_ge(score_ready, c + 1)
                then(dve.tensor_tensor(sfc[:, :, :], sc, eb_sb[:, :].unsqueeze(1).to_broadcast([P, CT, NE]), ALU.add))
                v = sfc[:, :, :].rearrange("p t (g e) -> p (t g) e", g=NG)
                dve.tensor_tensor(hi4[:, :, :], v[:, :, 0:4], v[:, :, 4:8], ALU.max)
                then(dve.tensor_tensor(lo4[:, :, :], v[:, :, 0:4], v[:, :, 4:8], ALU.min))
                dve.tensor_tensor(hi2[:, :, :], hi4[:, :, 0:2], hi4[:, :, 2:4], ALU.max)
                dve.tensor_tensor(lo2[:, :, :], hi4[:, :, 0:2], hi4[:, :, 2:4], ALU.min)
                then(dve.tensor_tensor(lo2b[:, :, :], lo4[:, :, 0:2], lo4[:, :, 2:4], ALU.max))
                then(dve.tensor_tensor(lo2[:, :, :], lo2[:, :, :], lo2b[:, :, :], ALU.max))
                dve.tensor_tensor(top1[:, :], hi2[:, :, 0], hi2[:, :, 1], ALU.max)
                dve.tensor_tensor(sec1[:, :], hi2[:, :, 0], hi2[:, :, 1], ALU.min)
                then(dve.tensor_tensor(sec2[:, :], lo2[:, :, 0], lo2[:, :, 1], ALU.max))
                then(dve.tensor_tensor(sec1[:, :], sec1[:, :], sec2[:, :], ALU.max))
                then(dve.tensor_tensor(gsx[:, :, TOPG:], top1[:, :].rearrange("p (t g) -> p t g", g=NG),
                                       sec1[:, :].rearrange("p (t g) -> p t g", g=NG), ALU.add))
                for t in range(CT):
                    last = dve.max(gtop[:, t, :], gsx[:, t, :])
                then(last)
                for t in range(CT):
                    last = dve.match_replace(gtaken[:, t, :], gtop[:, t, :], gsx[:, t, :], -BIG)
                then(last)
                then(dve.tensor_scalar(gmask[:, :].rearrange("p (t g) -> p t g", g=NG), gtaken[:, :, TOPG:], -BIG, None,
                                       ALU.is_equal))
                then(dve.tensor_tensor(masked[:, :, :].rearrange("p t (g e) -> p (t g) e", g=NG), v,
                                       gmask[:, :].unsqueeze(2).to_broadcast([P, CT * NG, GE]), ALU.mult))
                for t in range(CT):
                    last = dve.max(etop[:, t, :], masked[:, t, :])
                then(last)
                for t in range(CT):
                    last = dve.match_replace(taken[:, t, :], etop[:, t, :], masked[:, t, :], -BIG)
                then(last)
                dve.tensor_reduce(anyc[:, c, :], taken[:, :, :].rearrange("p t e -> p e t"), AX.X, ALU.min)
                then(dve.scalar_tensor_tensor(wsel[:, :, :], taken[:, :, :], -BIG, sc, ALU.is_equal, ALU.mult))
                then(dve.tensor_reduce(wsum[:, :], wsel[:, :, :], AX.X, ALU.add))
                then(dve.tensor_scalar(wsum[:, :], wsum[:, :], 1e-20, None, ALU.add))
                then(dve.reciprocal(winv[:, :], wsum[:, :]))
                then(dve.tensor_scalar(winv[:, :], winv[:, :], SCALE, None, ALU.mult))
                if c >= 2:
                    dve.wait_ge(coeft_ps_ready, c - 1)
                dve.tensor_tensor(coef[:, c % 2, :, :], wsel[:, :, :],
                                  winv[:, :].unsqueeze(2).to_broadcast([P, CT, NE]), ALU.mult).then_inc(coef_ready, 1)
            dve.tensor_scalar(used[:, :, :], anyc[:, :, :], -BIG, None, ALU.is_equal).then_inc(used_ready, 1)
            dve.wait_ge(used_ps_ready, 1)
            dve.tensor_scalar(act_c[:, :], listing[0:NE, 0:1], 0.5, None, ALU.is_gt).then_inc(active_ready, 1)
            dve.wait_ge(rank_ps_ready, 1)
            then(dve.tensor_copy(rk[:, 0:2], listing[0:NE, 8:10]))
            then(dve.tensor_tensor(rk[:, 2:3], rk[:, 1:2], rk[:, 0:1], ALU.subtract))
            then(dve.tensor_tensor(rk[:, 2:3], rk[:, 2:3], cst[0:NE, C_EIDX:C_EIDX + 1], ALU.add))
            then(dve.tensor_tensor(rk[:, 3:4], rk[:, 0:1], rk[:, 2:3], ALU.subtract))
            then(dve.tensor_tensor(rk[:, 3:4], rk[:, 3:4], act_c[:, :], ALU.mult))
            then(dve.tensor_tensor(rk[:, 4:5], rk[:, 3:4], rk[:, 2:3], ALU.add))
            dve.tensor_scalar(place[:, :], cst[0:NE, C_IOTA:C_IOTA + NE], rk[:, 4:5], None, ALU.is_equal)\
               .then_inc(place_ready, 1)
            dve.tensor_copy(nact[:, :], rk[0:1, 1:2]).then_inc(order_ready, 1)
            dve.wait_ge(order_ps_ready, 1)
            dve.tensor_copy(order[0:1, 0:NE], listing[0:1, 64:64 + NE]).then_inc(order_ready, 1)

            def split_low(h, k, b):
                s = H[h]
                dve.wait_ge(s["w_h_ready"], k)
                dve.tensor_tensor(w_l[b][:, :], raw[:, :], w_h[b][:, :].bitcast(F32), ALU.subtract)\
                   .then_inc(s["w_l_ready"], 1)

            def low(h, n, b):
                s = H[h]
                dve.wait_ge(s["hh_ready"], n + 1)
                dve.tensor_tensor(hl[b % 2][:, :], ht[b % 2][:, :], hh[b % 2][:, :].bitcast(F32), ALU.subtract)\
                   .then_inc(s["hl_ready"], 1)

            def times_up(h, n, b):
                s = H[h]
                if isinstance(n, int) and n < 2:
                    if h == 1:
                        dve.wait_ge(H[0]["h_ready"], last_n + (n + 3))
                else:
                    dve.wait_ge(s["h_ready"], n - 1)
                dve.wait_ge(s["silu_ready"], n + 1)
                dve.wait_ge(s["u_ready"], n + 1)
                dve.tensor_tensor(mt[b % 2][:, :], gu_ps[:, 2 * (b % 2) + 1, :], sg[b % 2][:, :], ALU.mult)\
                   .then_inc(s["m_ready"], 1)

            def pair(h, k, nxt, after=None):
                for b in range(HB):
                    n = k * HB + b
                    times_up(h, n, b)
                    low(h, n - 1, (b - 1) % HB)
                    if b == 2:
                        split_low(h, k + 1, nxt)
                    if after is not None:
                        after(b)

            def scale_code(h, g):
                if h == 1 and g == 0:
                    dve.wait_ge(H[0]["res_out"], 16 * HB)
                dve.wait_ge(H[h]["gback_ready"], g + 1)
                dve.tensor_tensor(res[:, g * BLK:(g + 1) * BLK], y_ps[:, g, :], s_sb[:, blocks_of(h, g)], ALU.mult)\
                   .then_inc(H[h]["gs_ready"], 1)

            def add_input(h, g):
                at = slice(g * BLK, (g + 1) * BLK)
                dve.wait_ge(H[h]["gs_ready"], g + 1)
                dve.tensor_tensor(res[:, at], res[:, at], x_sb[:, blocks_of(h, g)], ALU.add)\
                   .then_inc(H[h]["res_ready"], 1)

            def rest_of_half(h, after=None):
                pair(h, 1, 1, after)
                later_pairs(dve, n_pairs, lambda k, i, u: pair(h, k, u % 2))

            times_up(0, 0, 0)
            times_up(0, 1, 1)
            low(0, 0, 0)
            times_up(0, 2, 2)
            low(0, 1, 1)
            times_up(0, 3, 3)
            low(0, 2, 2)
            split_low(0, 1, 0)
            dve.wait_ge(order_ready, 2)
            n_pairs = pairs(dve.value_load(nact[0:1, 0:1], min_val=1, max_val=NE))
            last_n = n_pairs * HB
            rest_of_half(0)
            times_up(1, 0, 0)
            low(0, last_n + 3, 3)
            times_up(1, 1, 1)
            low(1, 0, 0)
            scale_code(0, 0)
            scale_code(0, 1)
            times_up(1, 2, 2)
            low(1, 1, 1)
            scale_code(0, 2)
            split_low(1, 1, 0)
            times_up(1, 3, 3)
            low(1, 2, 2)
            scale_code(0, 3)
            rest_of_half(1, lambda b: add_input(0, b))
            scale_code(1, 0)
            low(1, last_n + 3, 3)
            add_input(1, 0)
            for g in range(1, HB):
                scale_code(1, g)
                add_input(1, g)

        @block.gpsimd
        def _(pool):
            pool.memset(ones[:, :], 1.0).then_inc(pool_step, 1)
            pool.wait_ge(pool_step, 1)
            pool.wait_ge(mm_ready, 1)
            pool.partition_all_reduce(mmr[:, :], mm2[:, :], P, bass.bass_isa.ReduceOp.max).then_inc(mmr_ready, 1)
            def weigh(h, n, b, b_cb):
                s = H[h]
                if isinstance(n, int) and n < 2:
                    if h == 1:
                        pool.wait_ge(H[0]["hl_ready"], last_n + (n + 3))
                else:
                    pool.wait_ge(s["hl_ready"], n - 1)
                pool.wait_ge(s["m_ready"], n + 1)
                by = ones[:, :] if b_cb is None else cb[b_cb][:, b * BLK:(b + 1) * BLK]
                pool.tensor_tensor(ht[b % 2][:, :], mt[b % 2][:, :], by, ALU.mult).then_inc(s["h_ready"], 1)

            def pair(h, k, b_cb):
                for b in range(HB):
                    weigh(h, k * HB + b, b, b_cb)

            for h in range(2):
                s = H[h]
                pair(h, 0, None)
                if h == 0:
                    pool.wait_ge(order_ready, 2)
                    n_pairs = pairs(pool.value_load(nact[0:1, 0:1], min_val=1, max_val=NE))
                    last_n = n_pairs * HB
                pool.wait_ge(s["cb_in0"], 32)
                pair(h, 1, 0)

                def one(k, i, u):
                    b_cb = 1 - u % 2
                    pool.wait_ge(s[f"cb_in{b_cb}"], i * (16 * UN) + 32 * (u // 2 + u % 2 + 1))
                    pair(h, k, b_cb)

                later_pairs(pool, n_pairs, one)


def _constants():
    import numpy as np
    a = [[1, 1, 1, 0, 1, 1, 1, 0, 0, 0, 1, 1], [1, 1, 0, 1, 1, 1, 0, 0, 0, 1, 1, 0],
         [1, 0, 1, 1, 1, 0, 0, 0, 1, 1, 0, 1], [0, 1, 1, 1, 0, 0, 0, 1, 1, 0, 1, 1],
         [0, 0, 0, 0, 1, 1, 1, 1, 1, 1, 1, 1], [1, 1, 1, 1, 0, 0, 0, 0, 0, 0, 0, 0],
         [0, 0, 0, 0, 1, 1, 1, 1, 0, 0, 0, 0], [1, 1, 0, 0, 1, 1, 0, 0, 1, 1, 0, 0],
         [1, 0, 1, 0, 1, 0, 1, 0, 1, 0, 1, 0], [0, 1, 0, 1, 0, 1, 0, 1, 0, 1, 0, 1],
         [1, 0, 0, 1, 1, 0, 0, 1, 1, 0, 0, 1], [0, 1, 1, 0, 0, 1, 1, 0, 0, 1, 1, 0]]
    check = np.concatenate([np.array(a, np.float32).T, np.eye(CHECK, dtype=np.float32)], axis=1)
    c = np.zeros((P, NCONST), np.float32)
    c[:, C_IDENT:C_IDENT + P] = np.eye(P)
    k, i = np.arange(D)[:, None], np.arange(D)[None, :]
    turn = 2 * np.pi * ((k * i) % D) / D
    amp = np.where((k == 0) | (k == D // 2), np.sqrt(1 / D), np.sqrt(2 / D))
    c[:, C_DFT:C_DFT + D] = amp * np.where(k <= D // 2, np.cos(turn), np.sin(turn))
    for q in range(4):
        r = 32 * q
        c[r:r + CODE, C_HB + r:C_HB + r + CHECK] = check.T
        c[r:r + CHECK, C_WB + r:C_WB + r + CHECK] = 1
    c[:NE, C_TRI:C_TRI + NE] = np.arange(NE)[:, None] < np.arange(NE)[None, :]
    c[:, C_IOTA:C_IOTA + NE] = np.arange(NE)
    ka = np.minimum(np.arange(D), D - np.arange(D)).astype(np.float32) / np.float32(D) + np.float32(1e-8)
    c[:, C_KA] = ka
    c[:, C_KA2] = ka * ka
    c[:NE, C_EIDX] = np.arange(NE)
    c[:, C_ONE] = 1
    lx = np.log(np.array(SCALES, np.float64))
    n = len(SCALES)
    c[:, C_LX:C_LX + n] = -(n * lx - lx.sum()) / (n * (lx * lx).sum() - lx.sum() ** 2)
    return c


def kernel(L0_attn_x, L0_attn_W_el, L0_attn_b_el, L0_attn_W_le, L0_attn_b_le, L0_ffn_router_w, L0_ffn_e_bias,
           L0_ffn_Wg, L0_ffn_Wu, L0_ffn_Wd, L0_ffn_SWg, L0_ffn_SWu, L0_ffn_SWd):
    import numpy as np
    import concourse.bacc as bacc
    from concourse.bass_utils import run_bass_kernel_spmd

    x = np.ascontiguousarray(L0_attn_x)
    wle_pad = np.zeros((P, 4, D), x.dtype)
    bel_col = np.zeros((P, 1), x.dtype)
    for q in range(4):
        wle_pad[32 * q:32 * q + CODE, q] = L0_attn_W_le
        wle_pad[32 * q + CODE, q] = L0_attn_b_le
        bel_col[32 * q:32 * q + CODE, 0] = L0_attn_b_el
        bel_col[32 * q + CODE, 0] = 1
    arrays = {
        "x": x.reshape(-1, D),
        "const": _constants(),
        "w_el": np.ascontiguousarray(L0_attn_W_el),
        "wle_pad": wle_pad.reshape(P, 4 * D),
        "bel_col": bel_col,
        "router_t": np.ascontiguousarray(np.asarray(L0_ffn_router_w).T),
        "e_bias": np.asarray(L0_ffn_e_bias).reshape(1, NE),
        "wgu": np.stack([L0_ffn_Wg, L0_ffn_Wu], axis=2),
        "wd": np.ascontiguousarray(L0_ffn_Wd),
        "shared": np.concatenate([L0_ffn_SWg, L0_ffn_SWu, L0_ffn_SWd], axis=1),
    }
    nc = bacc.Bacc("TRN2", target_bir_lowering=False, num_devices=1)
    args = {n: nc.dram_tensor(f"in_{n}", a.shape, mybir.dt.from_np(a.dtype), kind="ExternalInput").ap()
            for n, a in arrays.items()}
    out = nc.dram_tensor("out_y", arrays["x"].shape, F32, kind="ExternalOutput").ap()
    recurrent_block_kernel(nc, out=out, **args)
    r = run_bass_kernel_spmd(nc, [{f"in_{n}": a for n, a in arrays.items()}], core_ids=[0])
    return r.results[0]["out_y"].reshape(x.shape)
```

```python
from contextlib import ExitStack

import concourse.bass as bass
from concourse import mybir

ALU = mybir.AluOpType
ACT = mybir.ActivationFunctionType
AX = mybir.AxisListType
F32 = mybir.dt.float32
F32R = mybir.dt.float32r
BF16 = mybir.dt.bfloat16
I32 = mybir.dt.int32

P = 128
D = 128
CODE = 24
CHECK = 12
NE = 64
NG = 8
GE = NE // NG
TOPG = 4
DI = 64
PAIR = 2
NPAIR = NE // PAIR
SCALE = 2.5
LN_EPS = 1e-5
FD_EPS = 1e-10
SCALES = (2, 4, 8, 16, 32)
BIG = 3.0e38
SIG_HALF = 2.0 ** -24
BIT = 16

C_IDENT = 0
C_DFT = 128
C_HB = 256
C_WB = 384
C_TRI = 512
C_IOTA = 576
C_KA = 640
C_KA2 = 641
C_EIDX = 642
C_ONE = 643
C_LX = 644
C_NRM = 649
C_NEGT = 654
C_PAT = 655
C_FOLD = 656
NCONST = 720


def recurrent_block_kernel(nc, x, const, w_el, wle_pad, bel_col, router_t, e_bias, wgu, wd, shared, out):
    T = x.shape[0]
    NT = T // P
    NCH = 4
    CT = NT // NCH
    RT = NT // 2
    QT = NT // 4
    BLK = 512
    TB = BLK // P
    NB = T // BLK
    HALF = T // 2
    HB = HALF // BLK
    UN = 4

    x_rows = x.rearrange("(p j) e -> p (j e)", j=NT)
    out_rows = out.rearrange("(p j) e -> p (j e)", j=NT)
    coef_dram = nc.dram_tensor("coef_by_expert", [NE, T], F32).ap()

    with ExitStack() as ctx:
        def sb(name, shape, dt=F32):
            return ctx.enter_context(nc.sbuf_tensor(name, shape, dt))

        def sem(name):
            return ctx.enter_context(nc.semaphore(name))

        gu_ps = ctx.enter_context(nc.psum_tensor("gu_ps", [P, 4, BLK], F32))
        y_ps = ctx.enter_context(nc.psum_tensor("y_ps", [P, 4, BLK], F32))

        x_sb = sb("x_sb", [P, NT * D])
        cst = sb("cst", [P, NCONST])
        wel_sb = sb("wel_sb", [P, CODE])
        wle_sb = sb("wle_sb", [P, 4 * D])
        bel_sb = sb("bel_sb", [P, 1])
        bel_t = sb("bel_t", [P, 1])
        rt_sb = sb("rt_sb", [P, NE])
        eb_sb = sb("eb_sb", [P, NE])
        bn6 = sb("bn6", [P, NT, 6])
        mv = sb("mv", [P, NT, 2])
        std = sb("std", [P, NT])
        rstd = sb("rstd", [P, NT])
        xn = sb("xn", [P, NT * D])
        xh = sb("xh", [P, T], F32R)
        xl = sb("xl", [P, T], F32R)
        nmr = sb("nmr", [P, NT])
        ext = sb("ext", [P, 2, NT])
        mm2 = sb("mm2", [P, 2])
        mmr = sb("mmr", [P, 2])
        den = sb("den", [1, 2])
        sums = sb("sums", [1, 8])
        mean = sb("mean", [1, 8])
        cnt = sb("cnt", [1, 8])
        lns = sb("lns", [1, 8])
        dimc = sb("dimc", [P, 2])
        ang = sb("ang", [P, 16])
        dft_f = sb("dft_f", [P, D])
        circ = sb("circ", [P, D])
        circ_h = sb("circ_h", [P, D], F32R)
        circ_l = sb("circ_l", [P, D], F32R)
        cel = sb("cel", [P, CODE])
        cel_h = sb("cel_h", [P, 4, D], F32R)
        cel_l = sb("cel_l", [P, 4, D], F32R)
        hb_bf = sb("hb_bf", [P, P], BF16)
        wb_bf = sb("wb_bf", [P, P], BF16)
        bits = sb("bits", [P, 2 * BLK], BF16)
        syn = sb("syn", [P, 2 * BLK], BF16)
        sgn = sb("sgn", [P, 2 * BLK], BF16)
        pat = sb("pat", [P, 2 * BLK], BF16)
        corr = sb("corr", [P, 2 * BLK], F32R)
        wle_h = sb("wle_h", [P, 4 * D], F32R)
        wle_l = sb("wle_l", [P, 4 * D], F32R)
        s_t = sb("s_t", [P, T])
        rt_h = sb("rt_h", [P, NE], F32R)
        rt_l = sb("rt_l", [P, NE], F32R)
        score = sb("score", [P, NT, NE])
        sfc = sb("sfc", [P, NT, NE])
        hi4 = sb("hi4", [P, RT * NG, 4])
        lo4 = sb("lo4", [P, RT * NG, 4])
        hi2 = sb("hi2", [P, RT * NG, 2])
        lo2 = sb("lo2", [P, RT * NG, 2])
        lo2b = sb("lo2b", [P, RT * NG, 2])
        top1 = sb("top1", [P, RT * NG])
        sec1 = sb("sec1", [P, RT * NG])
        sec2 = sb("sec2", [P, RT * NG])
        gsx = sb("gsx", [P, RT, TOPG + NG])
        gtop = sb("gtop", [P, RT, 8])
        gtaken = sb("gtaken", [P, RT, TOPG + NG])
        gmask = sb("gmask", [P, RT * NG])
        masked = xn[:, CT * D:RT * D].rearrange("p (t e) -> p t e", e=NE)
        etop = sb("etop", [P, RT, 8])
        taken = sb("taken", [P, RT, NE])
        wsel = sb("wsel", [P, RT, NE])
        wsum = sb("wsum", [P, RT])
        winv = sb("winv", [P, RT])
        coef = sb("coef", [P, NT, NE])
        coef_t = sfc[:, :, :].rearrange("p (c t) e -> p c (t e)", c=NCH)
        uses = sb("uses", [P, NCH])
        warm = sb("warm", [P, 1])
        act_c = sb("act_c", [NE, 1])
        rk = sb("rk", [NE, 3])
        place = sb("place", [NE, NE])
        order = sb("order", [1, NE + 4 * UN * PAIR], I32)
        nact = sb("nact", [1, 1], I32)
        WP = 3 * D
        raw = sb("raw", [P, WP])
        sraw = sb("sraw", [P, WP])
        sw_h = sb("sw_h", [P, WP], F32R)
        sw_l = sb("sw_l", [P, WP], F32R)
        w_h = [sb(f"w_h{b}", [P, WP], F32R) for b in range(2)]
        w_l = [sb(f"w_l{b}", [P, WP], F32R) for b in range(2)]
        cb = [sb(f"cb{b}", [P, HALF]) for b in range(2)]
        blk = cb[0][0:1, 0:SCALES[-1] ** 2]
        ends = [sum(sc * sc for sc in SCALES[:i]) for i in range(len(SCALES) + 1)]
        beside = [cb[1][0:1, a:b] for a, b in zip(ends, ends[1:])]
        ones = sb("ones", [P, BLK])
        sg = [sb(f"sg{b}", [P, BLK]) for b in range(2)]
        mt = [sb(f"mt{b}", [P, BLK]) for b in range(2)]
        ht = [sb(f"ht{b}", [P, BLK]) for b in range(2)]
        hh = [sb(f"hh{b}", [P, BLK], F32R) for b in range(2)]
        hl = [sb(f"hl{b}", [P, BLK], F32R) for b in range(2)]
        res = xn[:, 0:HALF]
        gt = xn[:, HALF:T].rearrange("p (b n) -> p b n", n=BLK)

        ident = cst[:, C_IDENT:C_IDENT + P]
        dft = cst[:, C_DFT:C_DFT + D]

        x_in = [sem(f"x_in{g}") for g in range(NB)]
        cst_in = sem("cst_in")
        rt_in = sem("rt_in")
        small_in = sem("small_in")
        dve_step = sem("dve_step")
        act_step = sem("act_step")
        pool_step = sem("pool_step")
        zero_ready = sem("zero_ready")
        ones_ready = sem("ones_ready")
        bel_ready = sem("bel_ready")
        var_ready = sem("var_ready")
        std_ready = sem("std_ready")
        rstd_ready = sem("rstd_ready")
        xn_dve_ready = sem("xn_dve_ready")
        xn_act_ready = sem("xn_act_ready")
        xt_ready = sem("xt_ready")
        xh_ready = sem("xh_ready")
        xfull_ready = sem("xfull_ready")
        xl_ready = sem("xl_ready")
        rt_h_ready = sem("rt_h_ready")
        rt_l_ready = sem("rt_l_ready")
        logit_ready = sem("logit_ready")
        score_ready = sem("score_ready")
        sfc_ready = sem("sfc_ready")
        mm_ready = sem("mm_ready")
        mmr_ready = sem("mmr_ready")
        den_ready = sem("den_ready")
        blk_ready = sem("blk_ready")
        sums_ready = sem("sums_ready")
        cnt_ready = sem("cnt_ready")
        ln_ready = sem("ln_ready")
        dim_ps_ready = sem("dim_ps_ready")
        dimc_ready = sem("dimc_ready")
        ang_ready = sem("ang_ready")
        sin_ready = sem("sin_ready")
        dftf_ready = sem("dftf_ready")
        circ_ps_ready = sem("circ_ps_ready")
        circ_ready = sem("circ_ready")
        circ_h_ready = sem("circ_h_ready")
        circ_l_ready = sem("circ_l_ready")
        cel_ps_ready = sem("cel_ps_ready")
        cel_ready = sem("cel_ready")
        cel_h_ready = sem("cel_h_ready")
        cel_l_ready = sem("cel_l_ready")
        hbwb_ready = sem("hbwb_ready")
        wle_h_ready = sem("wle_h_ready")
        wle_l_ready = sem("wle_l_ready")
        lat_ready = sem("lat_ready")
        bits_ready = sem("bits_ready")
        syn_ps_ready = sem("syn_ps_ready")
        syn_ready = sem("syn_ready")
        wt_ps_ready = sem("wt_ps_ready")
        pat_ready = sem("pat_ready")
        diff_ready = sem("diff_ready")
        corr_ready = sem("corr_ready")
        s_ps_ready = sem("s_ps_ready")
        s_ready = sem("s_ready")
        winv_ready = sem("winv_ready")
        coef_ready = [sem(f"coef_ready{r}") for r in range(2)]
        coeft_ps_ready = sem("coeft_ps_ready")
        coeft_ready = sem("coeft_ready")
        coeft_out = [sem(f"coeft_out{c}") for c in range(NCH)]
        used_ps_ready = sem("used_ps_ready")
        active_ready = sem("active_ready")
        rank_ps_ready = sem("rank_ps_ready")
        place_ready = sem("place_ready")
        order_ps_ready = sem("order_ps_ready")
        order_ready = sem("order_ready")
        sw_h_ready = sem("sw_h_ready")
        sw_l_ready = sem("sw_l_ready")
        H = []
        for h in range(2):
            H.append({n: sem(f"{n}_{h}") for n in (
                "raw_in", "cb_in0", "cb_in1", "w_h_ready", "w_l_ready", "g_ready", "u_ready", "silu_ready",
                "m_ready", "h_ready", "hh_ready", "hl_ready", "down_done", "gt_ready", "gback_ready",
                "gs_ready", "res_ready", "res_out")})

        block = ctx.enter_context(nc.Block())
        listing = y_ps[:, 3, :]
        S_BANK = (2, 3, 0, 1, 0, 1, 2, 3)

        def tile(buf, j):
            return buf[:, j * D:(j + 1) * D]

        def blocks_of(h, b):
            return slice(h * HALF + b * BLK, h * HALF + (b + 1) * BLK)

        def pairs(n_active):
            return (n_active + 1) // 2

        def later_pairs(eng, n_pairs, body):
            def step(i, u):
                k = i * UN + (u + 2)
                with eng.If(k <= n_pairs):
                    body(k, i, u)
                    if u + 1 < UN:
                        step(i, u + 1)

            half = NPAIR // UN // 2
            with eng.Fori(0, NPAIR // UN, half) as first:
                with eng.If(first * UN + 2 <= n_pairs):
                    with eng.Fori(first, first + half) as i:
                        step(i, 0)

        @block.sync
        def _(sp):
            w = TB * D
            for g in range(NB):
                sp.dma_start(x_sb[:, g * w:(g + 1) * w], x_rows[:, g * w:(g + 1) * w]).then_inc(x_in[g], 16)
                if g == 5:
                    sp.dma_start(cst[:, :], const).then_inc(cst_in, 16)
                    sp.dma_start(rt_sb[:, :], router_t).then_inc(rt_in, 16)
            for dst, src in ((wel_sb, w_el), (wle_sb, wle_pad), (bel_sb, bel_col), (sraw, shared)):
                sp.dma_start(dst[:, :], src).then_inc(small_in, 16)
            sp.dma_start(eb_sb[:, :], e_bias.to_broadcast([P, NE])).then_inc(small_in, 16)
            by_tile = coef_dram.rearrange("e (c t a p) -> e c t a p", c=NCH, a=2, p=P)
            for c in range(NCH):
                sp.wait_ge(coeft_ready, c + 1)
                for a in range(2):
                    sp.dma_start(by_tile[:, c, :, a, :],
                                 coef_t[a * NE:(a + 1) * NE, c, :].rearrange("e (t p) -> e t p", p=P)
                                 ).then_inc(coeft_out[c], 16)
            sp.wait_ge(order_ready, 2)
            n_pairs = pairs(sp.value_load(nact[0:1, 0:1], min_val=1, max_val=NE))

            def experts(k):
                return [sp.value_load(order[0:1, bass.ds(PAIR * (k - 1) + m, 1)], min_val=0, max_val=NE - 1)
                        for m in range(PAIR)]

            gate_up = raw[:, 0:2 * D].rearrange("p (what m i) -> p m what i", what=2, m=PAIR)

            def load_weights(h, chosen):
                s = H[h]
                for m, e in enumerate(chosen):
                    pick = bass.ds(e, 1)
                    sp.dma_start(gate_up[:, m], wgu[pick].rearrange("a h w i -> (a h) w i")).then_inc(s["raw_in"], 16)
                    sp.dma_start(raw[m * DI:(m + 1) * DI, 2 * D:3 * D],
                                 wd[pick].rearrange("a i h -> (a i) h")).then_inc(s["raw_in"], 16)

            def load_coefs(h, chosen, b):
                for m, e in enumerate(chosen):
                    sp.dma_start(cb[b][m * DI:(m + 1) * DI, :],
                                 coef_dram[bass.ds(e, 1), h * HALF:(h + 1) * HALF].to_broadcast([DI, HALF])
                                 ).then_inc(H[h][f"cb_in{b}"], 16)

            def store_results(h):
                for g in range(HB):
                    sp.wait_ge(H[h]["res_ready"], g + 1)
                    at = slice(h * HALF + g * BLK, h * HALF + (g + 1) * BLK)
                    sp.dma_start(out_rows[:, at], res[:, g * BLK:(g + 1) * BLK]).then_inc(H[h]["res_out"], 16)

            for h in range(2):
                s = H[h]
                chosen = experts(1)
                if h == 1:
                    o = H[0]
                    sp.wait_ge(o["w_l_ready"], n_pairs + 1)
                load_weights(h, chosen)
                if h == 1:
                    sp.wait_ge(o["h_ready"], (n_pairs + 1) * HB)
                    sp.wait_ge(o["cb_in0"], (n_pairs + 2) // 2 * 32)
                    sp.wait_ge(o["cb_in1"], (n_pairs + 1) // 2 * 32)
                if h == 0:
                    for c in range(NCH):
                        sp.wait_ge(coeft_out[c], 32)
                load_coefs(h, chosen, 0)

                def load_next(k, b):
                    chosen = experts(k + 1)
                    sp.wait_ge(s["w_l_ready"], k)
                    load_weights(h, chosen)
                    sp.wait_ge(s["h_ready"], k * HB)
                    load_coefs(h, chosen, b)

                load_next(1, 1)
                if h == 1:
                    store_results(0)
                later_pairs(sp, n_pairs, lambda k, i, u: load_next(k, u % 2))
            store_results(1)
            for h in range(2):
                sp.wait_ge(H[h]["res_out"], 16 * HB)

        @block.tensor
        def _(pe):
            def mm3(out_ap, lhs, rhs, start=True):
                (lh, ll), (rh, rl) = lhs, rhs
                pe.matmul(out_ap, ll, rh, start=start, stop=False, skip_group_check=True)
                pe.matmul(out_ap, lh, rl, start=False, stop=False, skip_group_check=True)
                return pe.matmul(out_ap, lh, rh, start=False, stop=True, skip_group_check=True)

            pe.wait_ge(cst_in, 16)

            def transposes(g):
                pe.wait_ge(xn_dve_ready, g + 1)
                pe.wait_ge(xn_act_ready, g + 1)
                if g >= 4:
                    pe.wait_ge(xfull_ready, g - 3)
                for t in range(TB):
                    last = pe.transpose(gu_ps[:, g % 4, t * P:(t + 1) * P], tile(xn, g * TB + t), ident)
                last.then_inc(xt_ready, 1)

            def logits(g):
                pe.wait_ge(xl_ready, g + 1)
                if g == 0:
                    pe.wait_ge(rt_l_ready, 1)
                for t in range(TB):
                    j = g * TB + t
                    at = j % CT * NE
                    last = mm3(y_ps[:, j // CT, at:at + NE], (tile(xh, j), tile(xl, j)), (rt_h[:, :], rt_l[:, :]))
                last.then_inc(logit_ready, 1)

            for g in range(4):
                transposes(g)
            for g in range(4):
                logits(g)
            for g in range(4, NB):
                transposes(g)
            for g in range(4, NB):
                logits(g)

            misc = gu_ps[:, 3, :]
            pe.wait_ge(xfull_ready, NB)
            pe.wait_ge(ln_ready, 1)
            n = len(SCALES)
            for i in range(n):
                last = pe.matmul(misc[:, 0:1], cst[0:1, C_LX + i:C_LX + i + 1].to_broadcast([1, P]), lns[0:1, i:i + 1],
                                 start=(i == 0), stop=(i == n - 1))
            last.then_inc(dim_ps_ready, 1)

            def turn_coefs(c):
                pe.wait_ge(score_ready, c + 1)
                for t in range(CT // 2):
                    j = c * CT + 2 * t
                    last = pe.transpose(y_ps[:, c, t * P:(t + 1) * P],
                                        coef[:, j:j + 2, :].rearrange("p t e -> p (t e)"), ident)
                last.then_inc(coeft_ps_ready, 1)

            pe.wait_ge(dftf_ready, 1)
            pe.matmul(misc[:, 128:256], dft_f[:, :], dft, start=True, stop=True).then_inc(circ_ps_ready, 1)
            pe.wait_ge(circ_ready, 1)
            pe.matmul(misc[:, 256:256 + CODE], circ[:, :], wel_sb[:, :], start=True, stop=True).then_inc(cel_ps_ready, 1)
            pe.wait_ge(cel_l_ready, 1)
            for c in range(2):
                for q in range(4):
                    at = slice(q * QT * P + c * BLK, q * QT * P + (c + 1) * BLK)
                    o = gu_ps[:, c, :]
                    pe.matmul(o, cel_l[:, q, :], xh[:, at], start=(q == 0), stop=False)
                    pe.matmul(o, cel_h[:, q, :], xl[:, at], start=False, stop=False)
                    last = pe.matmul(o, cel_h[:, q, :], xh[:, at], start=False, stop=(q == 3))
                last.then_inc(lat_ready, 1)
            pe.wait_ge(coef_ready[0], 1)
            turn_coefs(0)
            turn_coefs(1)
            pe.wait_ge(hbwb_ready, 1)
            for c in range(2):
                pe.wait_ge(bits_ready, c + 1)
                pe.matmul(gu_ps[:, 2 + c, :], hb_bf[:, :], bits[:, c * BLK:(c + 1) * BLK],
                          start=True, stop=True).then_inc(syn_ps_ready, 1)
            for c in range(2):
                pe.wait_ge(syn_ready, c + 1)
                pe.matmul(gu_ps[:, c, :], wb_bf[:, :], syn[:, c * BLK:(c + 1) * BLK],
                          start=True, stop=True).then_inc(wt_ps_ready, 1)
            def count_uses():
                pe.wait_ge(coeft_ready, NCH)
                for c in range(NCH):
                    last = pe.matmul(listing[0:NE, 0:1], cst[:, C_FOLD:C_FOLD + NE], uses[:, c:c + 1], start=(c == 0),
                                     stop=(c == NCH - 1))
                last.then_inc(used_ps_ready, 1)

            def rank():
                pe.wait_ge(active_ready, 1)
                pe.matmul(listing[0:NE, 8:9], cst[0:NE, C_TRI:C_TRI + NE], act_c[:, :], start=True, stop=True)
                every = cst[0:NE, C_ONE:C_ONE + 1].to_broadcast([NE, NE])
                pe.matmul(listing[0:NE, 9:10], every, act_c[:, :], start=True, stop=False)
                pe.matmul(listing[0:NE, 9:10], ident[0:NE, 0:NE], cst[0:NE, C_EIDX:C_EIDX + 1], start=False, stop=True)
                pe.matmul(listing[0:NE, 10:11], every, act_c[:, :], start=True, stop=True).then_inc(rank_ps_ready, 1)

            def list_experts():
                pe.wait_ge(place_ready, 1)
                pe.matmul(listing[0:1, 64:64 + NE], cst[0:NE, C_EIDX:C_EIDX + 1], place[:, :],
                          start=True, stop=True).then_inc(order_ps_ready, 1)

            pe.wait_ge(circ_l_ready, 1)
            pe.wait_ge(wle_l_ready, 1)

            def filtered(g):
                at = slice(g * BLK, (g + 1) * BLK)
                if g == 2:
                    pe.wait_ge(pat_ready, 2)
                if 4 <= g < 6:
                    pe.wait_ge(s_ready, g - 1)
                mm3(gu_ps[:, S_BANK[g], :], (circ_h[:, :], circ_l[:, :]), (xh[:, at], xl[:, at]))

            def decoded(g):
                q, c = g // 2, g % 2
                o = gu_ps[:, S_BANK[g], :]
                if g < 2:
                    pe.wait_ge(corr_ready, c + 1)
                cc = corr[:, c * BLK:(c + 1) * BLK]
                pe.matmul(o, wle_l[:, q * D:(q + 1) * D], cc, start=False, stop=False, skip_group_check=True)
                pe.matmul(o, wle_h[:, q * D:(q + 1) * D], cc, start=False, stop=True,
                          skip_group_check=True).then_inc(s_ps_ready, 1)

            for g in range(4):
                filtered(g)
            for g in range(NB):
                if g >= 4:
                    filtered(g)
                decoded(g)
                if g == 4:
                    for c in range(2, NCH):
                        pe.wait_ge(coef_ready[1], c - 1)
                        turn_coefs(c)
                elif g == 5:
                    count_uses()
                elif g == 6:
                    rank()
                elif g == 7:
                    list_experts()
            S = (sw_h, sw_l)
            W = [(w_h[b], w_l[b]) for b in range(2)]

            def down(h, n, b, w, first):
                s = H[h]
                pe.wait_ge(s["hl_ready"], n + 1)
                if first and h == 1:
                    pe.wait_ge(H[0]["res_ready"], b + 1)
                wh, wl = (v[:, 2 * D:3 * D] for v in w)
                mm3(y_ps[:, b, :], (wh, wl), (hh[b % 2][:, :], hl[b % 2][:, :]),
                    start=first).then_inc(s["down_done"], 1)

            def gate_up(h, n, b, w):
                s = H[h]
                if not isinstance(n, int) or n >= 2:
                    pe.wait_ge(s["m_ready"], n - 1)
                at = blocks_of(h, b)
                for what, name in ((0, "g_ready"), (1, "u_ready")):
                    wh, wl = (v[:, what * D:(what + 1) * D] for v in w)
                    mm3(gu_ps[:, 2 * (b % 2) + what, :], (wh, wl), (xh[:, at], xl[:, at])).then_inc(s[name], 1)

            def pair(h, k, w, before):
                for b in range(HB):
                    n = k * HB + b
                    gate_up(h, n, b, w)
                    if b >= 2:
                        down(h, n - 2, b - 2, w, False)
                    else:
                        down(h, n - 2, b + 2, before, before is S)

            def down_last(h, b):
                n = n_pairs * HB + b
                with pe.If((n_pairs % 2) > 0):
                    down(h, n, b, W[0], False)
                with pe.Else():
                    down(h, n, b, W[1], False)

            def turn_back(h, g):
                pe.wait_ge(H[h]["gs_ready"], g + 1)
                for t in range(TB):
                    last = pe.transpose(y_ps[:, g, t * P:(t + 1) * P], gt[:, g, t * P:(t + 1) * P], ident)
                last.then_inc(H[h]["gback_ready"], 1)

            def rest_of_half(h):
                s = H[h]
                pe.wait_ge(s["w_l_ready"], 1)
                pair(h, 1, W[0], S)

                def one(k, i, u):
                    pe.wait_ge(s["w_l_ready"], k)
                    pair(h, k, W[1 - u % 2], W[u % 2])

                later_pairs(pe, n_pairs, one)

            pe.wait_ge(sw_l_ready, 1)
            pe.wait_ge(s_ready, 6)
            gate_up(0, 0, 0, S)
            pe.wait_ge(s_ready, NB)
            gate_up(0, 1, 1, S)
            pe.wait_ge(order_ready, 2)
            gate_up(0, 2, 2, S)
            down(0, 0, 0, S, True)
            gate_up(0, 3, 3, S)
            down(0, 1, 1, S, True)
            n_pairs = pairs(pe.value_load(nact[0:1, 0:1], min_val=1, max_val=NE))
            rest_of_half(0)
            last_n = n_pairs * HB
            pe.wait_ge(H[0]["m_ready"], last_n + 3)
            gate_up(1, 0, 0, S)
            down_last(0, 2)
            pe.wait_ge(H[0]["m_ready"], last_n + 4)
            gate_up(1, 1, 1, S)
            down_last(0, 3)
            turn_back(0, 0)
            turn_back(0, 1)
            gate_up(1, 2, 2, S)
            turn_back(0, 2)
            down(1, 0, 0, S, True)
            gate_up(1, 3, 3, S)
            turn_back(0, 3)
            down(1, 1, 1, S, True)
            rest_of_half(1)
            down_last(1, 2)
            turn_back(1, 0)
            down_last(1, 3)
            for g in range(1, HB):
                turn_back(1, g)

        @block.scalar
        def _(act):
            steps = [0]

            def then(ins):
                steps[0] += 1
                ins.then_inc(act_step, 1)
                act.wait_ge(act_step, steps[0])

            def deviation(r):
                act.wait_ge(var_ready, r + 1)
                act.activation(std[:, r * RT:(r + 1) * RT], mv[:, r * RT:(r + 1) * RT, 1], ACT.Sqrt)\
                   .then_inc(std_ready, 1)

            def normalise(r):
                act.wait_ge(rstd_ready, r + 1)
                for g in range(r * HB, (r + 1) * HB):
                    for j in (g * TB + 2, g * TB + 3):
                        last = act.activation(tile(xn, j), tile(x_sb, j), ACT.Identity, bias=nmr[:, j:j + 1],
                                              scale=rstd[:, j:j + 1])
                    last.then_inc(xn_act_ready, 1)

            def high_x(g):
                act.wait_ge(xt_ready, g + 1)
                at = slice(g * BLK, (g + 1) * BLK)
                act.activation(xh[:, at], gu_ps[:, g % 4, :], ACT.Copy).then_inc(xh_ready, 1)
                act.activation(s_t[:, at], gu_ps[:, g % 4, :], ACT.Copy).then_inc(xfull_ready, 1)

            def sigmoids(c):
                act.wait_ge(logit_ready, 2 * c + 2)
                act.activation(score[:, c * CT:(c + 1) * CT, :].rearrange("p t e -> p (t e)"), y_ps[:, c, :],
                               ACT.Sigmoid).then_inc(score_ready, 1)

            deviation(0)
            normalise(0)
            act.wait_ge(rt_in, 16)
            act.activation(rt_h[:, :], rt_sb[:, :], ACT.Copy).then_inc(rt_h_ready, 1)
            high_x(0)
            high_x(1)
            deviation(1)
            high_x(2)
            high_x(3)
            normalise(1)
            for c in range(2):
                sigmoids(c)
            for g in range(4, NB):
                high_x(g)

            act.wait_ge(blk_ready, 1)
            for i, sc in enumerate(SCALES):
                last = act.activation(beside[i], blk[0:1, 0:sc * sc], ACT.Copy,
                                      accum_out=sums[0:1, i:i + 1])
            last.then_inc(sums_ready, 1)
            act.wait_ge(cnt_ready, 1)
            act.activation(lns[0:1, 0:5], cnt[0:1, 0:5], ACT.Ln).then_inc(ln_ready, 1)
            for c in range(2, NCH):
                sigmoids(c)
            act.wait_ge(small_in, 80)
            act.activation(wle_h[:, :], wle_sb[:, :], ACT.Copy).then_inc(wle_h_ready, 1)
            act.activation(sw_h[:, :], sraw[:, :], ACT.Copy).then_inc(sw_h_ready, 1)
            act.wait_ge(dim_ps_ready, 1)
            act.activation(dimc[:, 0:1], gu_ps[:, 3, 0:1], ACT.Copy).then_inc(dimc_ready, 1)
            act.wait_ge(ang_ready, 1)
            act.activation(ang[:, 6:8], ang[:, 4:6], ACT.Sin).then_inc(sin_ready, 1)
            act.activation(warm[:, :], cst[:, C_ONE:C_ONE + 1], ACT.Silu)
            act.wait_ge(circ_ps_ready, 1)
            act.activation(circ[:, :], gu_ps[:, 3, 128:256], ACT.Copy).then_inc(circ_ready, 1)
            act.wait_ge(circ_ready, 1)
            act.activation(circ_h[:, :], circ[:, :], ACT.Copy).then_inc(circ_h_ready, 1)
            act.wait_ge(cel_ps_ready, 1)
            act.wait_ge(zero_ready, 1)
            act.activation(cel[:, :], gu_ps[:, 3, 256:256 + CODE], ACT.Copy).then_inc(cel_ready, 1)
            for q in range(4):
                last = act.activation(cel_h[:, q, 32 * q:32 * q + CODE], gu_ps[:, 3, 256:256 + CODE], ACT.Copy)
            last.then_inc(cel_h_ready, 1)

            def copy_coefs(c):
                act.wait_ge(coeft_ps_ready, c + 1)
                act.activation(coef_t[:, c, :], y_ps[:, c, :], ACT.Copy, accum_out=uses[:, c:c + 1])\
                   .then_inc(coeft_ready, 1)

            act.wait_ge(bel_ready, 1)
            for c in range(2):
                at = slice(c * BLK, (c + 1) * BLK)
                act.wait_ge(lat_ready, c + 1)
                then(act.activation(sgn[:, at], gu_ps[:, c, :], ACT.Sign, bias=bel_t[:, 0:1]))
                act.activation(bits[:, at], sgn[:, at], ACT.Relu).then_inc(bits_ready, 1)
            for c in range(2):
                act.wait_ge(syn_ps_ready, c + 1)
                act.activation(syn[:, c * BLK:(c + 1) * BLK], gu_ps[:, 2 + c, :], ACT.Sign).then_inc(syn_ready, 1)
            for c in range(2):
                act.wait_ge(wt_ps_ready, c + 1)
                act.activation(pat[:, c * BLK:(c + 1) * BLK], gu_ps[:, c, :], ACT.Sign,
                               bias=cst[:, C_PAT:C_PAT + 1]).then_inc(pat_ready, 1)
            copy_coefs(0)
            copy_coefs(1)
            for c in range(2):
                at = slice(c * BLK, (c + 1) * BLK)
                act.wait_ge(diff_ready, c + 1)
                act.activation(corr[:, at], pat[:, at], ACT.Square, scale=0.5).then_inc(corr_ready, 1)
            for g in range(NB):
                if g == 5:
                    copy_coefs(2)
                    copy_coefs(3)
                act.wait_ge(s_ps_ready, g + 1)
                act.activation(s_t[:, g * BLK:(g + 1) * BLK], gu_ps[:, S_BANK[g], :], ACT.Copy).then_inc(s_ready, 1)

            def split_high(h, k, b):
                s = H[h]
                act.wait_ge(s["raw_in"], 64 * k)
                act.activation(w_h[b][:, :], raw[:, :], ACT.Copy).then_inc(s["w_h_ready"], 1)

            def high(h, n, b):
                s = H[h]
                if isinstance(n, int) and n < 2:
                    if h == 1:
                        act.wait_ge(H[0]["down_done"], last_n + (n + 3))
                else:
                    act.wait_ge(s["down_done"], n - 1)
                act.wait_ge(s["h_ready"], n + 1)
                act.activation(hh[b % 2][:, :], ht[b % 2][:, :], ACT.Copy).then_inc(s["hh_ready"], 1)

            def silu(h, n, b):
                s = H[h]
                act.wait_ge(s["g_ready"], n + 1)
                act.activation(sg[b % 2][:, :], gu_ps[:, 2 * (b % 2), :], ACT.Silu).then_inc(s["silu_ready"], 1)

            def pair(h, k, nxt):
                for b in range(HB):
                    n = k * HB + b
                    silu(h, n, b)
                    high(h, n - 1, (b - 1) % HB)
                    if b == 2:
                        if not isinstance(k, int) or k >= 2:
                            act.wait_ge(H[h]["down_done"], k * HB)
                        split_high(h, k + 1, nxt)

            def activate(h, g):
                act.wait_ge(H[h]["down_done"], last_n + (g + 1))
                act.activation(gt[:, g, :], y_ps[:, g, :], ACT.Silu).then_inc(H[h]["gt_ready"], 1)

            def rest_of_half(h):
                pair(h, 1, 1)
                later_pairs(act, n_pairs, lambda k, i, u: pair(h, k, u % 2))

            silu(0, 0, 0)
            silu(0, 1, 1)
            high(0, 0, 0)
            silu(0, 2, 2)
            high(0, 1, 1)
            split_high(0, 1, 0)
            silu(0, 3, 3)
            high(0, 2, 2)
            act.wait_ge(order_ready, 2)
            n_pairs = pairs(act.value_load(nact[0:1, 0:1], min_val=1, max_val=NE))
            last_n = n_pairs * HB
            rest_of_half(0)
            silu(1, 0, 0)
            high(0, last_n + 3, 3)
            activate(0, 0)
            activate(0, 1)
            silu(1, 1, 1)
            high(1, 0, 0)
            activate(0, 2)
            activate(0, 3)
            silu(1, 2, 2)
            high(1, 1, 1)
            split_high(1, 1, 0)
            silu(1, 3, 3)
            high(1, 2, 2)
            rest_of_half(1)
            activate(1, 0)
            high(1, last_n + 3, 3)
            for g in range(1, HB):
                activate(1, g)

        @block.vector
        def _(dve):
            steps = [0]

            def then(ins):
                steps[0] += 1
                ins.then_inc(dve_step, 1)
                dve.wait_ge(dve_step, steps[0])

            def stats(r):
                for g in range(r * HB, (r + 1) * HB):
                    dve.wait_ge(x_in[g], 16)
                    for j in range(g * TB, (g + 1) * TB):
                        last = dve.bn_stats(bn6[:, j, :], tile(x_sb, j))
                return last

            def variance(r):
                for j in range(r * RT, (r + 1) * RT):
                    last = dve.bn_aggr(mv[:, j, :], bn6[:, j, :])
                then(last)
                cs = slice(r * RT, (r + 1) * RT)
                dve.tensor_scalar(mv[:, cs, 1], mv[:, cs, 1], LN_EPS, None, ALU.add).then_inc(var_ready, 1)

            def extremes(c):
                v = x_sb[:, c * CT * D:(c + 1) * CT * D].rearrange("p (t d) -> p t d", d=D)
                dve.tensor_reduce(ext[:, 0, c * CT:(c + 1) * CT], v, AX.X, ALU.max)
                return dve.tensor_reduce(ext[:, 1, c * CT:(c + 1) * CT], v, AX.X, ALU.min)

            def normalise(r):
                cs = slice(r * RT, (r + 1) * RT)
                dve.wait_ge(std_ready, r + 1)
                then(dve.reciprocal(rstd[:, cs], std[:, cs]))
                then(dve.tensor_tensor(nmr[:, cs], rstd[:, cs], rstd[:, cs], ALU.mult))
                then(dve.tensor_tensor(nmr[:, cs], nmr[:, cs], mv[:, cs, 1], ALU.mult))
                then(dve.tensor_scalar(nmr[:, cs], nmr[:, cs], -0.5, 1.5, ALU.mult, ALU.add))
                then(dve.tensor_tensor(rstd[:, cs], rstd[:, cs], nmr[:, cs], ALU.mult))
                dve.scalar_tensor_tensor(nmr[:, cs], mv[:, cs, 0], -1.0, rstd[:, cs], ALU.mult, ALU.mult)\
                   .then_inc(rstd_ready, 1)
                for g in range(r * HB, (r + 1) * HB):
                    for j in (g * TB, g * TB + 1):
                        last = dve.tensor_scalar(tile(xn, j), tile(x_sb, j), mv[:, j, 0:1], rstd[:, j:j + 1],
                                                 ALU.subtract, ALU.mult)
                    last.then_inc(xn_dve_ready, 1)

            then(stats(0))
            variance(0)
            extremes(0)
            normalise(0)
            then(stats(1))
            variance(1)
            extremes(1)
            normalise(1)
            extremes(2)
            then(extremes(3))
            for i in range(2):
                last = dve.tensor_tensor(ext[:, i, :], ext[:, i, :], mv[:, :, 0], ALU.subtract)
            then(last)
            for i in range(2):
                last = dve.tensor_tensor(ext[:, i, :], ext[:, i, :], rstd[:, :], ALU.mult)
            then(last)
            dve.tensor_reduce(mm2[:, 0:1], ext[:, 0, :], AX.X, ALU.max)
            then(dve.tensor_reduce(mm2[:, 1:2], ext[:, 1, :], AX.X, ALU.min))
            dve.tensor_scalar(mm2[:, 1:2], mm2[:, 1:2], -1.0, None, ALU.mult).then_inc(mm_ready, 1)

            def spread():
                dve.wait_ge(mmr_ready, 1)
                then(dve.tensor_scalar(den[0:1, 0:1], mmr[0:1, 0:1], mmr[0:1, 1:2], FD_EPS, ALU.add, ALU.add))
                dve.reciprocal(den[0:1, 1:2], den[0:1, 0:1]).then_inc(den_ready, 1)

            def counts():
                dve.wait_ge(sums_ready, 1)
                then(dve.tensor_tensor(mean[0:1, 0:5], sums[0:1, 0:5], cst[0:1, C_NRM:C_NRM + 5], ALU.mult))
                for i, sc in enumerate(SCALES):
                    last = dve.tensor_scalar(beside[i], blk[0:1, 0:sc * sc], mean[0:1, i:i + 1], None,
                                             ALU.is_gt, ALU.add, accum_out=cnt[0:1, i:i + 1])
                then(last)
                dve.tensor_scalar(cnt[0:1, 0:5], cnt[0:1, 0:5], 1.0, None, ALU.max).then_inc(cnt_ready, 1)

            dve.wait_ge(zero_ready, 1)
            for r in range(2):
                sc = score[:, r * RT:(r + 1) * RT, :]
                biased = sfc[:, r * RT:(r + 1) * RT, :]
                v = biased.rearrange("p t (g e) -> p (t g) e", g=NG)
                dve.wait_ge(sfc_ready, r + 1)
                dve.tensor_tensor(hi4[:, :, :], v[:, :, 0:4], v[:, :, 4:8], ALU.max)
                then(dve.tensor_tensor(lo4[:, :, :], v[:, :, 0:4], v[:, :, 4:8], ALU.min))
                if r == 0:
                    spread()
                dve.tensor_tensor(hi2[:, :, :], hi4[:, :, 0:2], hi4[:, :, 2:4], ALU.max)
                dve.tensor_tensor(lo2[:, :, :], hi4[:, :, 0:2], hi4[:, :, 2:4], ALU.min)
                then(dve.tensor_tensor(lo2b[:, :, :], lo4[:, :, 0:2], lo4[:, :, 2:4], ALU.max))
                then(dve.tensor_tensor(lo2[:, :, :], lo2[:, :, :], lo2b[:, :, :], ALU.max))
                dve.tensor_tensor(top1[:, :], hi2[:, :, 0], hi2[:, :, 1], ALU.max)
                dve.tensor_tensor(sec1[:, :], hi2[:, :, 0], hi2[:, :, 1], ALU.min)
                then(dve.tensor_tensor(sec2[:, :], lo2[:, :, 0], lo2[:, :, 1], ALU.max))
                then(dve.tensor_tensor(sec1[:, :], sec1[:, :], sec2[:, :], ALU.max))
                then(dve.tensor_tensor(gsx[:, :, TOPG:], top1[:, :].rearrange("p (t g) -> p t g", g=NG),
                                       sec1[:, :].rearrange("p (t g) -> p t g", g=NG), ALU.add))
                for t in range(RT):
                    last = dve.max(gtop[:, t, :], gsx[:, t, :])
                then(last)
                if r == 0:
                    counts()
                for t in range(RT):
                    last = dve.match_replace(gtaken[:, t, :], gtop[:, t, :], gsx[:, t, :], -BIG)
                then(last)
                then(dve.tensor_scalar(gmask[:, :].rearrange("p (t g) -> p t g", g=NG), gtaken[:, :, TOPG:], -BIG, None,
                                       ALU.is_equal))
                then(dve.tensor_tensor(masked[:, :, :].rearrange("p t (g e) -> p (t g) e", g=NG), v,
                                       gmask[:, :].unsqueeze(2).to_broadcast([P, RT * NG, GE]), ALU.mult))
                for t in range(RT):
                    last = dve.max(etop[:, t, :], masked[:, t, :])
                then(last)
                for t in range(RT):
                    last = dve.match_replace(taken[:, t, :], etop[:, t, :], masked[:, t, :], -BIG)
                then(last)
                if r == 1:
                    dve.wait_ge(coef_ready[0], 1)
                then(dve.scalar_tensor_tensor(wsel[:, :, :], taken[:, :, :], -BIG, sc, ALU.is_equal, ALU.mult))
                then(dve.tensor_reduce(wsum[:, :], wsel[:, :, :], AX.X, ALU.add))
                then(dve.tensor_scalar(wsum[:, :], wsum[:, :], 1e-20, None, ALU.add))
                then(dve.reciprocal(winv[:, :], wsum[:, :]))
                last = dve.tensor_scalar(winv[:, :], winv[:, :], SCALE, None, ALU.mult)
                if r == 0:
                    last.then_inc(winv_ready, 1)
                else:
                    then(last)
                    for c in range(2):
                        at = slice(c * CT, (c + 1) * CT)
                        dve.tensor_tensor(coef[:, RT + c * CT:RT + (c + 1) * CT, :], wsel[:, at, :],
                                          winv[:, at].unsqueeze(2).to_broadcast([P, CT, NE]), ALU.mult)\
                           .then_inc(coef_ready[1], 1)
            dve.wait_ge(used_ps_ready, 1)
            dve.tensor_scalar(act_c[:, :], listing[0:NE, 0:1], 0.0, None, ALU.is_gt).then_inc(active_ready, 1)
            dve.wait_ge(rank_ps_ready, 1)
            dve.tensor_copy(nact[:, :], listing[0:1, 10:11]).then_inc(order_ready, 1)
            then(dve.tensor_scalar(rk[:, 0:1], listing[0:NE, 9:10], listing[0:NE, 8:9], None, ALU.subtract))
            then(dve.tensor_tensor(rk[:, 1:2], listing[0:NE, 8:9], rk[:, 0:1], ALU.subtract))
            then(dve.scalar_tensor_tensor(rk[:, 2:3], rk[:, 1:2], act_c[:, 0:1], rk[:, 0:1], ALU.mult, ALU.add))
            dve.tensor_scalar(place[:, :], cst[0:NE, C_IOTA:C_IOTA + NE], rk[:, 2:3], None, ALU.is_equal)\
               .then_inc(place_ready, 1)
            dve.wait_ge(order_ps_ready, 1)
            dve.tensor_copy(order[0:1, 0:NE], listing[0:1, 64:64 + NE]).then_inc(order_ready, 1)

            def split_low(h, k, b):
                s = H[h]
                dve.wait_ge(s["w_h_ready"], k)
                dve.tensor_tensor(w_l[b][:, :], raw[:, :], w_h[b][:, :].bitcast(F32), ALU.subtract)\
                   .then_inc(s["w_l_ready"], 1)

            def low(h, n, b):
                s = H[h]
                dve.wait_ge(s["hh_ready"], n + 1)
                dve.tensor_tensor(hl[b % 2][:, :], ht[b % 2][:, :], hh[b % 2][:, :].bitcast(F32), ALU.subtract)\
                   .then_inc(s["hl_ready"], 1)

            def times_up(h, n, b):
                s = H[h]
                if isinstance(n, int) and n < 2:
                    if h == 1:
                        dve.wait_ge(H[0]["h_ready"], last_n + (n + 3))
                else:
                    dve.wait_ge(s["h_ready"], n - 1)
                dve.wait_ge(s["silu_ready"], n + 1)
                dve.wait_ge(s["u_ready"], n + 1)
                dve.tensor_tensor(mt[b % 2][:, :], gu_ps[:, 2 * (b % 2) + 1, :], sg[b % 2][:, :], ALU.mult)\
                   .then_inc(s["m_ready"], 1)

            def pair(h, k, nxt):
                for b in range(HB):
                    n = k * HB + b
                    times_up(h, n, b)
                    low(h, n - 1, (b - 1) % HB)
                    if b == 2:
                        split_low(h, k + 1, nxt)

            def scale_code(h, g):
                dve.wait_ge(H[h]["gt_ready"], g + 1)
                dve.tensor_tensor(gt[:, g, :], gt[:, g, :], s_t[:, blocks_of(h, g)], ALU.mult)\
                   .then_inc(H[h]["gs_ready"], 1)

            def add_input(h, g):
                if h == 1 and g == 0:
                    dve.wait_ge(H[0]["res_out"], 16 * HB)
                dve.wait_ge(H[h]["gback_ready"], g + 1)
                dve.tensor_tensor(res[:, g * BLK:(g + 1) * BLK], y_ps[:, g, :], x_sb[:, blocks_of(h, g)], ALU.add)\
                   .then_inc(H[h]["res_ready"], 1)

            def rest_of_half(h):
                pair(h, 1, 1)
                later_pairs(dve, n_pairs, lambda k, i, u: pair(h, k, u % 2))

            times_up(0, 0, 0)
            times_up(0, 1, 1)
            low(0, 0, 0)
            times_up(0, 2, 2)
            low(0, 1, 1)
            split_low(0, 1, 0)
            times_up(0, 3, 3)
            low(0, 2, 2)
            dve.wait_ge(order_ready, 2)
            n_pairs = pairs(dve.value_load(nact[0:1, 0:1], min_val=1, max_val=NE))
            last_n = n_pairs * HB
            rest_of_half(0)
            times_up(1, 0, 0)
            low(0, last_n + 3, 3)
            scale_code(0, 0)
            scale_code(0, 1)
            times_up(1, 1, 1)
            low(1, 0, 0)
            scale_code(0, 2)
            scale_code(0, 3)
            add_input(0, 0)
            add_input(0, 1)
            times_up(1, 2, 2)
            low(1, 1, 1)
            add_input(0, 2)
            split_low(1, 1, 0)
            times_up(1, 3, 3)
            low(1, 2, 2)
            add_input(0, 3)
            rest_of_half(1)
            scale_code(1, 0)
            low(1, last_n + 3, 3)
            for g in range(1, HB):
                scale_code(1, g)
                add_input(1, g - 1)
            add_input(1, HB - 1)

        @block.gpsimd
        def _(pool):
            steps = [0]

            def then(ins):
                steps[0] += 1
                ins.then_inc(pool_step, 1)
                pool.wait_ge(pool_step, steps[0])

            pool.memset(cel_h[:, :, :].rearrange("p q c -> p (q c)").bitcast(F32), 0.0)
            pool.memset(cel_l[:, :, :].rearrange("p q c -> p (q c)").bitcast(F32), 0.0)
            pool.memset(order[:, :], 0)
            pool.memset(gsx[:, :, :], BIG).then_inc(zero_ready, 1)
            then(pool.memset(ones[:, :], 1.0))
            pool.wait_ge(rt_h_ready, 1)
            pool.tensor_tensor(rt_l[:, :], rt_sb[:, :], rt_h[:, :].bitcast(F32), ALU.subtract).then_inc(rt_l_ready, 1)
            def low_x(g):
                at = slice(g * BLK, (g + 1) * BLK)
                pool.wait_ge(xh_ready, g + 1)
                pool.wait_ge(xfull_ready, g + 1)
                pool.tensor_tensor(xl[:, at], s_t[:, at], xh[:, at].bitcast(F32), ALU.subtract)\
                    .then_inc(xl_ready, 1)

            for g in range(4):
                low_x(g)
            pool.wait_ge(small_in, 80)
            pool.wait_ge(cst_in, 16)
            pool.tensor_tensor(bel_t[:, :], bel_sb[:, :], cst[:, C_NEGT:C_NEGT + 1], ALU.add).then_inc(bel_ready, 1)
            pool.tensor_copy(hb_bf[:, :], cst[:, C_HB:C_HB + P])
            pool.tensor_copy(wb_bf[:, :], cst[:, C_WB:C_WB + P]).then_inc(hbwb_ready, 1)

            def bias_scores(r):
                pool.wait_ge(score_ready, 2 * (r + 1))
                at = slice(r * RT, (r + 1) * RT)
                pool.tensor_tensor(sfc[:, at, :], score[:, at, :], eb_sb[:, :].unsqueeze(1).to_broadcast([P, RT, NE]),
                                   ALU.add).then_inc(sfc_ready, 1)

            bias_scores(0)
            pool.wait_ge(mm_ready, 1)
            pool.partition_all_reduce(mmr[:, :], mm2[:, :], P, bass.bass_isa.ReduceOp.max).then_inc(mmr_ready, 1)
            low_x(4)
            low_x(5)
            pool.wait_ge(den_ready, 1)
            pool.wait_ge(xn_act_ready, 2)
            pool.tensor_scalar(blk[:, :], xn[0:1, 0:1024], mmr[0:1, 1:2], den[0:1, 1:2], ALU.add, ALU.mult)\
                .then_inc(blk_ready, 1)
            low_x(6)
            low_x(7)
            pool.wait_ge(dimc_ready, 1)
            then(pool.tensor_scalar(dimc[:, 1:2], dimc[:, 0:1], 1.0, 2.0, ALU.max, ALU.min))
            dcol, ka, ka2 = dimc[:, 1:2], cst[:, C_KA:C_KA + 1], cst[:, C_KA2:C_KA2 + 1]
            pool.tensor_scalar(ang[:, 0:1], dcol, 0.2, 1.0, ALU.mult, ALU.add)
            pool.tensor_scalar(ang[:, 1:2], dcol, 0.5, 1.0, ALU.mult, ALU.add)
            then(pool.tensor_scalar(ang[:, 2:3], dcol, 0.1, None, ALU.mult))
            pool.tensor_tensor(ang[:, 9:10], ang[:, 0:1], dcol, ALU.mult)
            pool.tensor_tensor(ang[:, 10:11], ang[:, 1:2], ka, ALU.mult)
            then(pool.tensor_tensor(ang[:, 3:4], ang[:, 2:3], ka2, ALU.mult))
            pool.tensor_tensor(ang[:, 8:9], ang[:, 9:10], ang[:, 10:11], ALU.add)
            then(pool.tensor_tensor(ang[:, 11:12], ang[:, 9:10], ka, ALU.subtract))
            then(pool.tensor_tensor(ang[:, 12:13], ang[:, 11:12], ang[:, 3:4], ALU.add))
            pool.tensor_scalar(ang[:, 4:5], ang[:, 8:9], -1.0, 3.14159265358979, ALU.mult, ALU.add)
            pool.tensor_scalar(ang[:, 5:6], ang[:, 12:13], -1.0, 1.5707963267949, ALU.mult, ALU.add)\
                .then_inc(ang_ready, 1)
            pool.wait_ge(sin_ready, 1)
            pool.tensor_scalar(dft_f[:, :], dft, ang[:, 6:7], ang[:, 7:8], ALU.mult, ALU.mult).then_inc(dftf_ready, 1)
            bias_scores(1)
            pool.wait_ge(cel_ready, 1)
            pool.wait_ge(cel_h_ready, 1)
            for q in range(4):
                at = slice(32 * q, 32 * q + CODE)
                last = pool.tensor_tensor(cel_l[:, q, at], cel[:, :], cel_h[:, q, at].bitcast(F32), ALU.subtract)
            last.then_inc(cel_l_ready, 1)
            pool.wait_ge(circ_h_ready, 1)
            pool.tensor_tensor(circ_l[:, :], circ[:, :], circ_h[:, :].bitcast(F32), ALU.subtract)\
                .then_inc(circ_l_ready, 1)
            pool.wait_ge(wle_h_ready, 1)
            pool.tensor_tensor(wle_l[:, :], wle_sb[:, :], wle_h[:, :].bitcast(F32), ALU.subtract)\
                .then_inc(wle_l_ready, 1)
            pool.wait_ge(winv_ready, 1)
            pool.tensor_tensor(coef[:, 0:RT, :], wsel[:, :, :], winv[:, :].unsqueeze(2).to_broadcast([P, RT, NE]),
                               ALU.mult).then_inc(coef_ready[0], 1)
            pool.wait_ge(sw_h_ready, 1)
            pool.tensor_tensor(sw_l[:, :], sraw[:, :], sw_h[:, :].bitcast(F32), ALU.subtract).then_inc(sw_l_ready, 1)
            for c in range(2):
                at = slice(c * BLK, (c + 1) * BLK)
                pool.wait_ge(bits_ready, c + 1)
                then(pool.tensor_scalar(sgn[:, at], bits[:, at], 2.0, -1.0, ALU.mult, ALU.add))
            for c in range(2):
                at = slice(c * BLK, (c + 1) * BLK)
                pool.wait_ge(pat_ready, c + 1)
                pool.tensor_tensor(pat[:, at], sgn[:, at], pat[:, at], ALU.subtract).then_inc(diff_ready, 1)

            def weigh(h, n, b, b_cb):
                s = H[h]
                if isinstance(n, int) and n < 2:
                    if h == 1:
                        pool.wait_ge(H[0]["hl_ready"], last_n + (n + 3))
                else:
                    pool.wait_ge(s["hl_ready"], n - 1)
                pool.wait_ge(s["m_ready"], n + 1)
                by = ones[:, :] if b_cb is None else cb[b_cb][:, b * BLK:(b + 1) * BLK]
                pool.tensor_tensor(ht[b % 2][:, :], mt[b % 2][:, :], by, ALU.mult).then_inc(s["h_ready"], 1)

            def pair(h, k, b_cb):
                for b in range(HB):
                    weigh(h, k * HB + b, b, b_cb)

            for h in range(2):
                s = H[h]
                pair(h, 0, None)
                if h == 0:
                    pool.wait_ge(order_ready, 2)
                    n_pairs = pairs(pool.value_load(nact[0:1, 0:1], min_val=1, max_val=NE))
                    last_n = n_pairs * HB
                pool.wait_ge(s["cb_in0"], 32)
                pair(h, 1, 0)

                def one(k, i, u):
                    b_cb = 1 - u % 2
                    pool.wait_ge(s[f"cb_in{b_cb}"], i * (16 * UN) + 32 * (u // 2 + u % 2 + 1))
                    pair(h, k, b_cb)

                later_pairs(pool, n_pairs, one)


def _constants():
    import numpy as np
    a = [[1, 1, 1, 0, 1, 1, 1, 0, 0, 0, 1, 1], [1, 1, 0, 1, 1, 1, 0, 0, 0, 1, 1, 0],
         [1, 0, 1, 1, 1, 0, 0, 0, 1, 1, 0, 1], [0, 1, 1, 1, 0, 0, 0, 1, 1, 0, 1, 1],
         [0, 0, 0, 0, 1, 1, 1, 1, 1, 1, 1, 1], [1, 1, 1, 1, 0, 0, 0, 0, 0, 0, 0, 0],
         [0, 0, 0, 0, 1, 1, 1, 1, 0, 0, 0, 0], [1, 1, 0, 0, 1, 1, 0, 0, 1, 1, 0, 0],
         [1, 0, 1, 0, 1, 0, 1, 0, 1, 0, 1, 0], [0, 1, 0, 1, 0, 1, 0, 1, 0, 1, 0, 1],
         [1, 0, 0, 1, 1, 0, 0, 1, 1, 0, 0, 1], [0, 1, 1, 0, 0, 1, 1, 0, 0, 1, 1, 0]]
    check = np.concatenate([np.array(a, np.float32).T, np.eye(CHECK, dtype=np.float32)], axis=1)
    c = np.zeros((P, NCONST), np.float32)
    c[:, C_IDENT:C_IDENT + P] = np.eye(P)
    k, i = np.arange(D)[:, None], np.arange(D)[None, :]
    turn = 2 * np.pi * ((k * i) % D) / D
    amp = np.where((k == 0) | (k == D // 2), np.sqrt(1 / D), np.sqrt(2 / D))
    c[:, C_DFT:C_DFT + D] = amp * np.where(k <= D // 2, np.cos(turn), np.sin(turn))
    for q in range(4):
        r = 32 * q
        c[r:r + CODE, C_HB + r:C_HB + r + CHECK] = check.T
        c[r:r + CHECK, C_WB + r:C_WB + r + CHECK] = BIT * np.eye(CHECK) - 1
    c[:NE, C_TRI:C_TRI + NE] = np.arange(NE)[:, None] < np.arange(NE)[None, :]
    c[:, C_IOTA:C_IOTA + NE] = np.arange(NE)
    ka = np.minimum(np.arange(D), D - np.arange(D)).astype(np.float32) / np.float32(D) + np.float32(1e-8)
    c[:, C_KA] = ka
    c[:, C_KA2] = ka * ka
    c[:NE, C_EIDX] = np.arange(NE)
    c[:, C_ONE] = 1
    lx = np.log(np.array(SCALES, np.float64))
    n = len(SCALES)
    c[:, C_LX:C_LX + n] = -(n * lx - lx.sum()) / (n * (lx * lx).sum() - lx.sum() ** 2)
    c[:, C_NRM:C_NRM + n] = [1 / (sc * sc) for sc in SCALES]
    c[:, C_NEGT] = -SIG_HALF
    c[:, C_PAT] = 3.5 - BIT
    c[:, C_FOLD:C_FOLD + NE] = np.arange(P)[:, None] % NE == np.arange(NE)[None, :]
    return c


def kernel(L0_attn_x, L0_attn_W_el, L0_attn_b_el, L0_attn_W_le, L0_attn_b_le, L0_ffn_router_w, L0_ffn_e_bias,
           L0_ffn_Wg, L0_ffn_Wu, L0_ffn_Wd, L0_ffn_SWg, L0_ffn_SWu, L0_ffn_SWd):
    import numpy as np
    import concourse.bacc as bacc
    from concourse.bass_utils import run_bass_kernel_spmd

    x = np.ascontiguousarray(L0_attn_x)
    wle_pad = np.zeros((P, 4, D), x.dtype)
    bel_col = np.zeros((P, 1), x.dtype)
    for q in range(4):
        wle_pad[32 * q:32 * q + CODE, q] = L0_attn_W_le
        wle_pad[32 * q + CODE, q] = L0_attn_b_le
        bel_col[32 * q:32 * q + CODE, 0] = L0_attn_b_el
        bel_col[32 * q + CODE, 0] = 1
    arrays = {
        "x": x.reshape(-1, D),
        "const": _constants(),
        "w_el": np.ascontiguousarray(L0_attn_W_el),
        "wle_pad": wle_pad.reshape(P, 4 * D),
        "bel_col": bel_col,
        "router_t": np.ascontiguousarray(np.asarray(L0_ffn_router_w).T),
        "e_bias": np.asarray(L0_ffn_e_bias).reshape(1, NE),
        "wgu": np.stack([L0_ffn_Wg, L0_ffn_Wu], axis=2),
        "wd": np.ascontiguousarray(L0_ffn_Wd),
        "shared": np.concatenate([L0_ffn_SWg, L0_ffn_SWu, L0_ffn_SWd], axis=1),
    }
    nc = bacc.Bacc("TRN2", target_bir_lowering=False, num_devices=1)
    args = {n: nc.dram_tensor(f"in_{n}", a.shape, mybir.dt.from_np(a.dtype), kind="ExternalInput").ap()
            for n, a in arrays.items()}
    out = nc.dram_tensor("out_y", arrays["x"].shape, F32, kind="ExternalOutput").ap()
    recurrent_block_kernel(nc, out=out, **args)
    r = run_bass_kernel_spmd(nc, [{f"in_{n}": a for n, a in arrays.items()}], core_ids=[0])
    return r.results[0]["out_y"].reshape(x.shape)
```
